# Optimizing a Trainium2 kernel written in Bass

```python
import numpy as np
import jax
import jax.numpy as jnp

def _softmax(x, axis=-1):
    return jax.nn.softmax(x, axis=axis)

def _gelu(x):
    return jax.nn.gelu(x, approximate=True)

def _silu(x):
    return jax.nn.silu(x)

def _sigmoid(x):
    return jax.nn.sigmoid(x)

def _layernorm(x, axis=-1, eps=1e-05):
    m = jnp.mean(x, axis=axis, keepdims=True)
    v = jnp.var(x, axis=axis, keepdims=True)
    return (x - m) / jnp.sqrt(v + eps)

def _scatter_add(tgt, idx, src, axis=0):
    return tgt.at[idx].add(src)

def _segment_sum(src, seg, n):
    return jax.ops.segment_sum(src, seg, n)
kernel_name = 'mk_flamingo_gated_d1_seqx_r2_7da47f'

def setup_inputs(seed: int=0):
    np.random.seed(seed)
    _w = jnp.asarray

    def _rec_inputs():
        import jax
        import jax.numpy as jnp
        _rk = jax.random.key(seed)
        x = -0.0002928 + 1 * jax.random.normal(jax.random.fold_in(_rk, 1), (16, 1024, 512), jnp.float32)
        _lenS = 1024 - jax.random.randint(jax.random.fold_in(_rk, 7), (16,), 0, max(1, 1024 // 4) + 1, jnp.int32)
        _lenS2 = 64 - jax.random.randint(jax.random.fold_in(_rk, 8), (16,), 0, max(1, 64 // 4) + 1, jnp.int32)
        _ctx_1024P = jax.random.normal(jax.random.fold_in(_rk, 11), (16, 16, 512), jnp.float32)
        _ctx_1024c = jax.random.dirichlet(jax.random.fold_in(_rk, 511), 0.3 * jnp.ones((16,), jnp.float32), (16, 64))
        _ctx_1024t = jnp.einsum('bsk,bkd->bsd', _ctx_1024c, _ctx_1024P)
        _ctx_1024t = _ctx_1024t * jax.lax.rsqrt(jnp.mean(jnp.square(_ctx_1024t)) + 1e-12) * 0.953939
        ctx_1024 = 2.81802e-05 + 1.00001 * (_ctx_1024t + 0.3 * jax.random.normal(jax.random.fold_in(_rk, 611), (16, 64, 512), jnp.float32))
        _validS = jnp.arange(1024)[None, :] < _lenS[:, None]
        _validS2 = jnp.arange(64)[None, :] < _lenS2[:, None]
        _causal = jnp.tril(jnp.ones((1024, 1024), dtype=bool))
        mask_BxS2_bk0 = jnp.logical_not(jnp.broadcast_to(_validS2[:, :], (16, 64)))
        _g = jax.random.normal(jax.random.fold_in(_rk, 9001), (2, 1), jnp.float32)
        _g = jnp.sign(_g) * jnp.maximum(jnp.abs(_g), 1.0) + (_g == 0) * 1.0
        g_xattn = _g[0]
        g_ffn = _g[1]
        return (x, ctx_1024, mask_BxS2_bk0, g_xattn, g_ffn)
    x, ctx_1024, mask_BxS2_bk0, g_xattn, g_ffn = _rec_inputs()

    def _L0_xattn_setup():
        import jax, jax.numpy as jnp
        import numpy as np
        NUM_HEADS, NUM_KV, HEAD_DIM, WIDTH = (4, 1, 128, 512)
        MASK_FILL = -2.3819763e+38

        def _apply_rope(x, positions, max_wavelength=10000.0):
            d = x.shape[-1]
            freq_exp = 2.0 / d * jnp.arange(d // 2, dtype=jnp.float32)
            timescale = max_wavelength ** freq_exp
            radians = positions[..., None].astype(jnp.float32) / timescale
            radians = radians[..., None, :]
            sin, cos = (jnp.sin(radians), jnp.cos(radians))
            x1, x2 = jnp.split(x, 2, axis=-1)
            out = jnp.concatenate([x1 * cos - x2 * sin, x2 * cos + x1 * sin], axis=-1)
            return out.astype(x.dtype)

        def _rmsnorm(x, scale):
            var = jnp.mean(jnp.square(x.astype(jnp.float32)), axis=-1, keepdims=True)
            normed = x * jax.lax.rsqrt(var + 1e-06)
            return (normed * (1 + scale)).astype(x.dtype)
        key = jax.random.key(seed)
        ks = jax.random.split(key, 7)
        B, T, S = (8, 256, 1024)
        return {'x': jax.random.normal(ks[0], (B, T, WIDTH), jnp.float32), 'mem_seq': jax.random.normal(ks[1], (B, S, WIDTH), jnp.float32), 'mem_mask': jax.random.randint(ks[2], (B, S), 0, 2).astype(bool), 'rms_scale': jax.random.normal(ks[3], (WIDTH,), jnp.float32) * 0.02, 'q_w': jax.random.normal(ks[4], (NUM_HEADS, WIDTH, HEAD_DIM), jnp.float32) / np.sqrt(WIDTH), 'kv_w': jax.random.normal(ks[5], (2, NUM_KV, WIDTH, HEAD_DIM), jnp.float32) / np.sqrt(WIDTH), 'out_w': jax.random.normal(ks[6], (NUM_HEADS, HEAD_DIM, WIDTH), jnp.float32) / np.sqrt(NUM_HEADS * HEAD_DIM)}
    _L0_xattn_all = _L0_xattn_setup()
    _L0_xattn_in = {k: v for k, v in _L0_xattn_all.items() if k in ('rms_scale', 'q_w', 'kv_w', 'out_w')}
    del _L0_xattn_all

    def _L0_ffn_setup():
        import jax, jax.numpy as jnp
        import numpy as np
        DM, NEXPERTS, SETS, ESIZE = (512, 32, 4, 32)
        B, S = (2, 4096)
        key = jax.random.key(seed)
        ks = jax.random.split(key, 7)
        sc = 0.02
        return {'x': jax.random.normal(ks[0], (B, S, DM), jnp.float32), 'Wc': jax.random.normal(ks[1], (DM, NEXPERTS, SETS), jnp.float32) * sc, 'bc': jax.random.normal(ks[2], (NEXPERTS, SETS), jnp.float32) * sc, 'W1': jax.random.normal(ks[3], (NEXPERTS, SETS, DM, ESIZE), jnp.float32) * sc, 'b1': jax.random.normal(ks[4], (NEXPERTS, SETS, ESIZE), jnp.float32) * sc, 'W2': jax.random.normal(ks[5], (NEXPERTS, SETS, DM, ESIZE), jnp.float32) * sc, 'b2': jax.random.normal(ks[6], (NEXPERTS, SETS, DM), jnp.float32) * sc}
    _L0_ffn_all = _L0_ffn_setup()
    _L0_ffn_in = {k: v for k, v in _L0_ffn_all.items() if k in ('Wc', 'bc', 'W1', 'b1', 'W2', 'b2')}
    del _L0_ffn_all
    return {'x': x, 'ctx_1024': ctx_1024, 'mask_BxS2_bk0': mask_BxS2_bk0, 'g_xattn': g_xattn, 'g_ffn': g_ffn, 'L0_xattn_rms_scale': _L0_xattn_in['rms_scale'], 'L0_xattn_q_w': _L0_xattn_in['q_w'], 'L0_xattn_kv_w': _L0_xattn_in['kv_w'], 'L0_xattn_out_w': _L0_xattn_in['out_w'], 'L0_ffn_Wc': _L0_ffn_in['Wc'], 'L0_ffn_bc': _L0_ffn_in['bc'], 'L0_ffn_W1': _L0_ffn_in['W1'], 'L0_ffn_b1': _L0_ffn_in['b1'], 'L0_ffn_W2': _L0_ffn_in['W2'], 'L0_ffn_b2': _L0_ffn_in['b2']}

def reference(x, ctx_1024, mask_BxS2_bk0, g_xattn, g_ffn, L0_xattn_rms_scale, L0_xattn_q_w, L0_xattn_kv_w, L0_xattn_out_w, L0_ffn_Wc, L0_ffn_bc, L0_ffn_W1, L0_ffn_b1, L0_ffn_W2, L0_ffn_b2):
    import jax
    import jax.numpy as jnp

    def _L0_xattn_ref(x, mem_seq, mem_mask, rms_scale, q_w, kv_w, out_w):
        import jax, jax.numpy as jnp
        import numpy as np
        NUM_HEADS, NUM_KV, HEAD_DIM, WIDTH = (4, 1, 128, 512)
        MASK_FILL = -2.3819763e+38

        def _apply_rope(x, positions, max_wavelength=10000.0):
            d = x.shape[-1]
            freq_exp = 2.0 / d * jnp.arange(d // 2, dtype=jnp.float32)
            timescale = max_wavelength ** freq_exp
            radians = positions[..., None].astype(jnp.float32) / timescale
            radians = radians[..., None, :]
            sin, cos = (jnp.sin(radians), jnp.cos(radians))
            x1, x2 = jnp.split(x, 2, axis=-1)
            out = jnp.concatenate([x1 * cos - x2 * sin, x2 * cos + x1 * sin], axis=-1)
            return out.astype(x.dtype)

        def _rmsnorm(x, scale):
            var = jnp.mean(jnp.square(x.astype(jnp.float32)), axis=-1, keepdims=True)
            normed = x * jax.lax.rsqrt(var + 1e-06)
            return (normed * (1 + scale)).astype(x.dtype)
        B, S, _ = mem_seq.shape
        T = x.shape[1]
        G = NUM_HEADS // NUM_KV
        xn = _rmsnorm(x, rms_scale)
        mn = _rmsnorm(mem_seq, rms_scale)
        q = jnp.einsum('BTD,NDH->BTNH', xn, q_w)
        kv = jnp.einsum('BSD,cKDH->cBSKH', mn, kv_w)
        k, v = (kv[0], kv[1])
        q_pos = jnp.broadcast_to(jnp.arange(S, T + S), (B, T))
        k_pos = jnp.broadcast_to(jnp.arange(S), (B, S))
        q = _apply_rope(q, q_pos) * HEAD_DIM ** (-0.5)
        k = _apply_rope(k, k_pos)
        q = q.reshape(B, T, NUM_KV, G, HEAD_DIM)
        logits = jnp.einsum('BTKGH,BSKH->BKGTS', q, k, preferred_element_type=jnp.float32)
        masked = jnp.where(mem_mask[:, None, None, None, :], logits, MASK_FILL)
        probs = jax.nn.softmax(masked, axis=-1).astype(x.dtype)
        enc = jnp.einsum('BKGTS,BSKH->BTKGH', probs, v).reshape(B, T, NUM_HEADS, HEAD_DIM)
        return jnp.einsum('BTNH,NHD->BTD', enc, out_w)

    def _L0_ffn_ref(x, Wc, bc, W1, b1, W2, b2):
        import jax, jax.numpy as jnp
        import numpy as np
        DM, NEXPERTS, SETS, ESIZE = (512, 32, 4, 32)
        B, S = (2, 4096)
        b, s, d = x.shape
        g = Wc.shape[1]
        grouped = x.reshape(b, s // g, g, d)
        logits = jnp.einsum('bntd,des->bntes', grouped, Wc) + bc
        tie = jnp.linspace(0.0, 1e-06, g, dtype=x.dtype).reshape(-1, 1, 1)
        logits = logits + tie
        perm = (logits == jnp.max(logits, axis=-3, keepdims=True)).astype(x.dtype)
        permuted = jnp.einsum('bntd,bntes->bnesd', grouped, perm)
        inner = jax.nn.relu(jnp.einsum('bnesd,esdf->bnesf', permuted, W1) + b1)
        result_permuted = jnp.einsum('bnesf,esdf->bnesd', inner, W2) + b2
        result = jnp.einsum('bnesd,bntes->bntd', result_permuted, perm)
        return result.reshape(b, s, d)
    x = x + jnp.tanh(g_xattn[0]) * _L0_xattn_ref(_layernorm(x, axis=-1), ctx_1024, mask_BxS2_bk0, L0_xattn_rms_scale, L0_xattn_q_w, L0_xattn_kv_w, L0_xattn_out_w)
    x = x + jnp.tanh(g_ffn[0]) * _L0_ffn_ref(_layernorm(x, axis=-1), L0_ffn_Wc, L0_ffn_bc, L0_ffn_W1, L0_ffn_b1, L0_ffn_W2, L0_ffn_b2)
    return x

_drawn_inputs = setup_inputs


def setup_inputs(seed=0):
    import zlib

    import numpy as np

    out = dict(_drawn_inputs(seed))
    spreads = {}
    factors = {'L0_xattn_rms_scale': 4.693, 'L0_ffn_b1': 22.25}
    for name, (base, spread) in spreads.items():
        noise = np.random.default_rng([zlib.crc32(name.encode()), seed]).standard_normal(out[name].shape)
        drawn = base * np.exp(spread * noise) if base else spread * noise
        out[name] = jnp.asarray(drawn.astype(out[name].dtype))
    for name, factor in factors.items():
        out[name] = (out[name] * factor).astype(out[name].dtype)
    return out
```

```python
from contextlib import ExitStack

import numpy as np

import concourse.bass as bass
from concourse import mybir
from concourse.alu_op_type import AluOpType as ALU

F32 = mybir.dt.float32
F32R = mybir.dt.float32r
BF16 = mybir.dt.bfloat16
U8 = mybir.dt.uint8
ACT = mybir.ActivationFunctionType
AX_X = mybir.AxisListType.X

P = 128
B, T, D = 16, 1024, 512
S = 64
H, DH = 4, 128
E, G = 128, 32
F = 32
C = D // P
NT = T // P
TH = NT // 2
HT = T // 2
GT = P // G
NG = T // G
Q = E // 4
QB = 4
FILL = -2.3819763e38
LN_EPS, RMS_EPS = 1e-5, 1e-6


class Steps:

    def __init__(self, sem, names):
        self.sem, self.per = sem, len(names)
        self.place = {n: k + 1 for k, n in enumerate(names)}
        assert len(self.place) == self.per

    def done(self, i, name, back=0):
        return i * self.per + (1 - back) * self.per + self.place[name]


class Slot:

    def __init__(self, sem, per):
        self.sem, self.per = sem, per

    def done(self, i, k=0, back=0):
        return i * (16 * self.per) + 16 * ((1 - back) * self.per + k + 1)


def run_steps(eng, steps, plan, rounds):
    def body(i):
        seen = {}

        def wait(who, name, back=0):
            at = who.done(0, name, back)
            if id(who) in seen:
                assert at <= seen[id(who)], (step, name)
                return
            seen[id(who)] = at
            eng.wait_ge(who.sem, who.done(i, name, back))
        for name, fn in plan:
            step = name
            seen.clear()
            last = fn(eng, i, wait)
            if steps is not None:
                last.then_inc(steps.sem, 1)
    if rounds == 1:
        body(0)
    else:
        with eng.Fori(0, rounds) as i:
            body(i)


def build(nc, x, ctx_in, mask, gx_in, gf_in, rms, q_w, kv_w, out_w, Wc, bc, W1, b1, W2, b2,
          ident_in, cos_in, sin_in, tie_in, gmask_in, out):
    x1_dram = nc.dram_tensor("x1_scratch", (B, T, D), F32, kind="Internal").ap()
    kr_dram = nc.dram_tensor("k_scratch", (B, P, 2 * S + 1), F32, kind="Internal").ap()
    vw_dram = nc.dram_tensor("vw_scratch", (B, P, 2, D), F32, kind="Internal").ap()

    top = ExitStack()

    def sem(name):
        return top.enter_context(nc.semaphore(name))

    with top:
        ps = top.enter_context(nc.psum_tensor("ps", [P, 8, 512], F32))
        sb0 = lambda n, s, dt=F32: top.enter_context(nc.sbuf_tensor(n, s, dt))
        w1 = sb0("w1", [P, C, E * F])
        ident = sb0("ident", [P, P])
        nhalf = sb0("nhalf", [P, 8])
        none_ = sb0("neg_one", [P, 8])
        eps_l = sb0("eps_layer", [P, 8])
        eps_r = sb0("eps_rms", [P, 8])
        small = (nhalf, none_, eps_l, eps_r)
        gate_x = sb0("gate_x", [P, 1])
        gate_f = sb0("gate_f", [P, 1])
        s_w1 = sem("s_w1")
        attn = ExitStack()
        with attn:
            sba = lambda n, s, dt=F32: attn.enter_context(nc.sbuf_tensor(n, s, dt))
            cos = sba("cos", [P, S + T])
            sin = sba("sin", [P, S + T])
            qh = sba("qh", [P, C, D], F32R)
            ql = sba("ql", [P, C, D], F32R)
            prologue(nc, sem, ps, w1, ident, small, gate_x, gate_f, cos, sin, qh, ql, s_w1,
                     ctx_in, mask, gx_in, gf_in, rms, q_w, kv_w, out_w, W1,
                     ident_in, cos_in, sin_in, kr_dram, vw_dram)
            attention(nc, sem, ps, ident, small, cos, sin, qh, ql, x, kr_dram, vw_dram, x1_dram)
        experts(nc, sem, ps, w1, ident, small, gate_f, s_w1, Wc, bc, b1, b2, tie_in, gmask_in,
                x1_dram, W2, out)


def prologue(nc, sem, ps, w1, ident, small, gate_x, gate_f, cos, sin, qh, ql, s_w1,
             ctx_in, mask, gx_in, gf_in, rms, q_w, kv_w, out_w, W1,
             ident_in, cos_in, sin_in, kr_dram, vw_dram):
    nhalf, none_, eps_l, eps_r = small
    st = ExitStack()
    with st:
        sb = lambda n, s, dt=F32: st.enter_context(nc.sbuf_tensor(n, s, dt))
        NC = B * S // P
        cx = sb("cx", [P, NC, D])
        mnT = sb("mnT", [P, C, B * S])
        vT = sb("vT", [P, B * S])
        kr = sb("kr", [P, B, 2 * S + 1])
        kt = sb("kt", [P, 2, HT])
        ow = sb("ow", [P, H, D])
        qraw = sb("qraw", [P, C, H, DH])
        kvraw = sb("kvraw", [P, C, 2 * DH])
        kvs = sb("kvs", [P, C, 3 * DH])
        vwb = sb("vwb", [P, 2, 2, D])
        rs1 = sb("rs1", [P, C])
        mk = sb("mk", [P, B], U8)
        mkf = sb("mkf", [P, B])
        bst = sb("bst", [P, NC, 6])
        mv = sb("mv", [P, NC, 2])
        ms = sb("ms", [P, NC])
        ms2 = sb("ms2", [P, NC])
        rr = sb("rr", [P, NC])
        gts = sb("gts", [P, 2])

        names = ["ctx", "small", "qw", "kvw", "ow", "tab"]
        L = {n: sem(f"p_{n}") for n in names}
        s_vws = [sem(f"p_vws{k}") for k in range(2)]
        s_krs = sem("p_krs")
        count = {}

        cT = [("cT", c, h) for c in range(C) for h in range(2)]
        kj = [("k", w, h) for w in range(2) for h in range(2)]
        vj = [("v", h) for h in range(2)]
        vwj = [("vw", b, pr) for b in range(B) for pr in range(2)]
        pe_names = cT + kj + vj + vwj
        act_names = (["gate"] + [("cn", t) for t in range(NC)] + [("mn",) + n[1:] for n in cT]
                     + [("vT", h) for h in range(2)] + [("vwe", b, pr) for b in range(B) for pr in range(2)])
        rope = [(o, h) for h in range(2) for o in ("kC", "sS", "k0", "sC", "kS", "k1")]
        dve_names = (["sc1"] + [("st", t) for t in range(NC)] + [("ag", t) for t in range(NC)]
                     + [("qs", c) for c in range(C)] + ["qhi", "qlo"]
                     + [("kvs", c) for c in range(C)] + [("ks1", c) for c in range(C)] + [("ks2", c) for c in range(C)]
                     + ["mkf", "mkb"] + rope)
        pool_names = ["nh", "ms0", "ms1", "ms2", "ms3"]
        PE, AC, DV, PO = (Steps(sem(f"p_{n}s"), l) for n, l in
                          (("pe", pe_names), ("act", act_names), ("dve", dve_names), ("pool", pool_names)))

        blk = st.enter_context(nc.Block())

        @blk.sync
        def _(e):
            def load(name, *pairs):
                for o, s in pairs:
                    e.dma_start(o, s).then_inc(L[name], 16)
                    count[name] = count.get(name, 0) + 16
            for s in (PE, AC, DV, PO):
                e.sem_inc(s.sem, s.per)
            load("small", (rs1[:], rms),
                 (gts[:, 0:1], gx_in.partition_broadcast(P)), (gts[:, 1:2], gf_in.partition_broadcast(P)),
                 (mk[0:S, :], mask), (mk[S:P, :], mask),
                 (ident[:], ident_in))
            load("ctx", (cx[:], ctx_in.rearrange("b s d -> (b s) d").rearrange("(n p) d -> p n d", p=P)))
            load("kvw", *[(kvraw[:, :, k * DH:(k + 1) * DH], kv_w[k, 0].rearrange("(c p) h -> p c h", p=P)) for k in range(2)])
            load("qw", *[(qraw[:, :, n, :], q_w[n].rearrange("(c p) h -> p c h", p=P)) for n in range(H)])
            load("tab", (cos[:], cos_in), (sin[:], sin_in))
            load("ow", (ow[:], out_w.rearrange("n h d -> h n d")))

            def store_vw(b):
                e.wait_ge(AC.sem, AC.done(0, ("vwe", b, 1)))
                e.dma_start(vw_dram[b], vwb[:, b % 2]).then_inc(s_vws[b % 2], 16)
            e.wait_ge(DV.sem, DV.done(0, ("k1", 1)))
            e.dma_start(kr_dram.rearrange("b p k -> p b k"), kr[:]).then_inc(s_krs, 16)
            for b in range(B):
                store_vw(b)
            e.dma_start(w1[:], W1).then_inc(s_w1, 16)
            e.wait_ge(s_krs, 16)
            for s in s_vws:
                e.wait_ge(s, 16 * B // 2)

        def pool_plan():
            def nh(e, i, w):
                for t, v in ((none_, -1.0), (eps_l, LN_EPS), (eps_r, RMS_EPS)):
                    e.memset(t[:], v)
                return e.memset(nhalf[:], -0.5)
            yield "nh", nh

            def m0(e, i, w):
                w(DV, ("ag", NC - 1))
                return e.tensor_tensor(ms[:], mv[:, :, 0], mv[:, :, 0], ALU.mult)
            yield "ms0", m0

            def m1(e, i, w):
                w(PO, "ms0")
                return e.tensor_tensor(ms2[:], ms[:], mv[:, :, 1], ALU.add)
            yield "ms1", m1

            def m2(e, i, w):
                w(PO, "ms1")
                return e.tensor_tensor(ms[:], ms2[:], eps_r[:, 0:NC], ALU.add)
            yield "ms2", m2

            def m3(e, i, w):
                w(PO, "ms2")
                return e.tensor_tensor(rr[:], ms[:], nhalf[:, 0:NC], ALU.pow)
            yield "ms3", m3

        @blk.gpsimd
        def _(e):
            run_steps(e, PO, list(pool_plan()), 1)

        def act_plan():
            def gate(e, i, w):
                e.wait_ge(L["small"], count["small"])
                e.activation(gate_x[:], gts[:, 0:1], ACT.Tanh)
                return e.activation(gate_f[:], gts[:, 1:2], ACT.Tanh)
            yield "gate", gate
            for t in range(NC):
                def cn(e, i, w, t=t):
                    w(PO, "ms3")
                    return e.activation(cx[:, t, :], cx[:, t, :], ACT.Copy, scale=rr[:, t:t + 1])
                yield ("cn", t), cn
            for _, c, h in cT:
                def mn(e, i, w, c=c, h=h):
                    w(PE, ("cT", c, h))
                    return e.activation(mnT[:, c, h * HT:(h + 1) * HT], ps[:, 2 * c + h, :], ACT.Copy)
                yield ("mn", c, h), mn
            for h in range(2):
                def v(e, i, w, h=h):
                    w(PE, ("v", h))
                    return e.activation(vT[:, h * HT:(h + 1) * HT], ps[:, 4 + h, :], ACT.Copy)
                yield ("vT", h), v
            for b in range(B):
                for pr in range(2):
                    def vwe(e, i, w, b=b, pr=pr):
                        w(PE, ("vw", b, pr))
                        if b >= 2 and pr == 0:
                            e.wait_ge(s_vws[b % 2], 16 * (b // 2))
                        if b == 0:
                            w(AC, "gate")
                        return e.activation(vwb[:, b % 2, pr, :], ps[:, 6 + pr, :], ACT.Copy, scale=gate_x[:])
                    yield ("vwe", b, pr), vwe

        @blk.scalar
        def _(e):
            run_steps(e, AC, list(act_plan()), 1)

        def dve_plan():
            def sc1(e, i, w):
                e.wait_ge(L["small"], count["small"])
                return e.tensor_scalar(rs1[:], rs1[:], 1.0, None, ALU.add)
            yield "sc1", sc1
            for t in range(NC):
                def s_(e, i, w, t=t):
                    e.wait_ge(L["ctx"], count["ctx"])
                    return e.bn_stats(bst[:, t, :], cx[:, t, :])
                yield ("st", t), s_
            for t in range(NC):
                def a_(e, i, w, t=t):
                    w(DV, ("st", t))
                    return e.bn_aggr(mv[:, t, :], bst[:, t, :])
                yield ("ag", t), a_
            for c in range(C):
                def qs(e, i, w, c=c):
                    e.wait_ge(L["qw"], count["qw"])
                    w(DV, "sc1")
                    v = qraw[:, c].rearrange("p n h -> p (n h)")
                    return e.tensor_scalar(v, v, rs1[:, c:c + 1], None, ALU.mult)
                yield ("qs", c), qs
            qf = qraw[:].rearrange("p c n h -> p (c n h)")

            def qhi(e, i, w):
                w(DV, ("qs", C - 1))
                return e.tensor_copy(qh[:].rearrange("p c n -> p (c n)"), qf)
            yield "qhi", qhi

            def qlo(e, i, w):
                w(DV, "qhi")
                return e.tensor_tensor(ql[:].rearrange("p c n -> p (c n)"), qf,
                                       qh[:].rearrange("p c n -> p (c n)").bitcast(F32), ALU.subtract)
            yield "qlo", qlo
            for c in range(C):
                def kv(e, i, w, c=c):
                    e.wait_ge(L["kvw"], count["kvw"])
                    return e.tensor_scalar(kvs[:, c, 0:2 * DH], kvraw[:, c, :], rs1[:, c:c + 1], None, ALU.mult)
                yield ("kvs", c), kv
            HH = DH // 2
            for k in range(2):
                for c in range(C):
                    def ks(e, i, w, c=c, k=k):
                        return e.tensor_scalar(kvs[:, c, 2 * DH + k * HH:2 * DH + (k + 1) * HH],
                                               kvraw[:, c, (1 - k) * HH:(2 - k) * HH], rs1[:, c:c + 1], None, ALU.mult)
                    yield (f"ks{k + 1}", c), ks
            yield "mkf", lambda e, i, w: e.tensor_copy(mkf[:], mk[:])

            def mkb(e, i, w):
                w(DV, "mkf")
                return e.tensor_scalar(kr[:, :, 2 * S], mkf[:], -FILL, FILL, ALU.mult, ALU.add)
            yield "mkb", mkb
            nb = HT // S
            for h in range(2):
                def tab(t):
                    return t[:, 0:S].unsqueeze(1).broadcast_to([P, nb, S])
                def krv(k):
                    return kr[:, h * nb:(h + 1) * nb, k * S:(k + 1) * S]
                def psv(w_, h=h):
                    return ps[:, 2 * w_ + h, :].rearrange("p (b s) -> p b s", s=S)
                kv0 = kt[:, 0, :].rearrange("p (b s) -> p b s", s=S)
                kv1 = kt[:, 1, :].rearrange("p (b s) -> p b s", s=S)
                k0v, k1v = krv(0), krv(1)

                def f1(e, i, w, h=h, o=kv0, a=psv(0), t=tab(cos)):
                    w(PE, ("k", 1, h))
                    e.wait_ge(L["tab"], count["tab"])
                    if h:
                        w(DV, ("k1", h - 1))
                    return e.tensor_tensor(o, a, t, ALU.mult)
                yield ("kC", h), f1
                yield ("sS", h), lambda e, i, w, h=h, o=kv1, a=psv(1), t=tab(sin): e.tensor_tensor(o, a, t, ALU.mult)

                def f3(e, i, w, h=h, o=k0v, a=kv0, b=kv1):
                    w(DV, ("sS", h))
                    return e.tensor_tensor(o, a, b, ALU.subtract)
                yield ("k0", h), f3

                def f4(e, i, w, h=h, o=kv0, a=psv(1), t=tab(cos)):
                    w(DV, ("k0", h))
                    return e.tensor_tensor(o, a, t, ALU.mult)
                yield ("sC", h), f4
                yield ("kS", h), lambda e, i, w, h=h, o=kv1, a=psv(0), t=tab(sin): e.tensor_tensor(o, a, t, ALU.mult)

                def f6(e, i, w, h=h, o=k1v, a=kv0, b=kv1):
                    w(DV, ("kS", h))
                    return e.tensor_tensor(o, a, b, ALU.add)
                yield ("k1", h), f6

        @blk.vector
        def _(e):
            run_steps(e, DV, list(dve_plan()), 1)

        def pe_plan():
            for _, c, h in cT:
                def f(e, i, w, c=c, h=h):
                    e.wait_ge(L["small"], count["small"])
                    w(AC, ("cn", 4 * h + 3))
                    for t in range(4):
                        last = e.transpose(ps[:, 2 * c + h, t * P:(t + 1) * P], cx[:, 4 * h + t, c * P:(c + 1) * P], ident[:])
                    return last
                yield ("cT", c, h), f
            for _, k, h in kj:
                def f(e, i, w, k=k, h=h):
                    w(AC, ("mn", C - 1, 1)); w(DV, ("ks2", C - 1))
                    for c in range(C):
                        last = e.matmul(ps[:, 2 * k + h, :], kvs[:, c, 2 * DH * k:2 * DH * k + DH],
                                        mnT[:, c, h * HT:(h + 1) * HT], start=(c == 0), stop=(c == C - 1))
                    return last
                yield ("k", k, h), f
            for _, h in vj:
                def f(e, i, w, h=h):
                    for c in range(C):
                        last = e.matmul(ps[:, 4 + h, :], kvs[:, c, DH:2 * DH],
                                        mnT[:, c, h * HT:(h + 1) * HT], start=(c == 0), stop=(c == C - 1))
                    return last
                yield ("v", h), f
            for _, b, pr in vwj:
                def f(e, i, w, b=b, pr=pr):
                    e.wait_ge(L["ow"], count["ow"])
                    w(AC, ("vwe", b - 1, pr) if b else ("vT", 1))
                    for n in range(2):
                        last = e.matmul(ps[n * S:(n + 1) * S, 6 + pr, :], vT[:, b * S:(b + 1) * S], ow[:, 2 * pr + n, :],
                                        start=True, stop=True)
                    return last
                yield ("vw", b, pr), f

        @blk.tensor
        def _(e):
            run_steps(e, PE, list(pe_plan()), 1)


def attention(nc, sem, ps, ident, small, cos, sin, qh, ql, x, kr_dram, vw_dram, x1_dram):
    nhalf, none_, eps_l, eps_r = small
    st = ExitStack()
    with st:
        sb = lambda n, s, dt=F32: st.enter_context(nc.sbuf_tensor(n, s, dt))
        xin = sb("xin", [P, NT, D])
        xo = sb("xo", [P, TH, D])
        xh = sb("xh", [P, TH, D])
        xTh = sb("xTh", [P, C, HT], F32R)
        xTl = sb("xTl", [P, C, HT], F32R)
        qc = sb("qc", [P, H, HT])
        qs = sb("qs", [P, H, HT])
        lt = sb("lt", [P, 2, HT])
        lg = sb("lg", [P, 2, 512])
        pr_ = sb("pr", [P, 2, 512])
        pT = sb("pT", [P, 2, 512])
        kb = sb("kb", [P, 2 * S + 1])
        vw = sb("vw", [P, 2, D])
        bst = sb("a_bst", [P, NT, 6])
        junk = sb("a_junk", [P, 1])
        mv = sb("a_mv", [P, NT, 2])
        va = sb("va", [P, 2, TH])
        r1 = sb("r1", [P, 2, TH])
        vb = sb("vb", [P, 2, TH])
        vc = sb("vc", [P, 2, TH])
        r2 = sb("r2", [P, 2, TH])
        sc = sb("sc", [P, 2, TH])
        nb = sb("nb", [P, 2, TH])
        mx = sb("mx", [P, 2, 8])
        sm = sb("sm", [P, 2, 8])
        rc = sb("rc", [P, 2, 8])

        halves = range(2)
        pairs = [(h, tp) for h in halves for tp in range(TH // 2)]

        def pe_names():
            for h in halves:
                yield from (("T", h, c) for c in range(C))
                yield from (("Q", h, n) for n in range(H))
                yield from (("L", h, p) for p in range(2))
                yield from (("LT", h, tp) for tp in range(2))
                for tp in range(2):
                    yield ("PT", h, tp)
                    yield from (("PV", h, t) for t in (2 * tp, 2 * tp + 1))

        def act_names():
            for h in halves:
                yield from (("xh", h, t) for t in range(TH))
                yield from (("hi", h, c) for c in range(C))
                yield from (("lt", h, p) for p in range(2))
                yield from (("ex", h, tp) for tp in range(2))
                yield from (("pT", h, tp) for tp in range(2))

        def dve_names():
            for h in halves:
                for t in range(TH):
                    yield ("st", h, t)
                yield from (("ag", h, t) for t in range(TH))
            for h in halves:
                yield from (("lo", h, c) for c in range(C))
                yield from ((o, h, n) for n in range(H) for o in ("qc", "qs"))
                yield from (("mx", h, tp) for tp in range(2))
                yield from (("sb", h, tp) for tp in range(2))
                for tp in range(2):
                    yield ("sm", h, tp)
                    yield ("rc", h, tp)
                yield from (("rs", h, t) for t in range(TH))

        def pool_names():
            for h in halves:
                yield from ((o, h) for o in ("va", "r1", "vb", "vc", "vd", "r2", "sc", "ns", "nb"))
            for h in halves:
                yield from (("pr", h, tp) for tp in range(2))

        PE, AC, DV, PO = (Steps(sem(f"a_{n}s"), list(l())) for n, l in
                          (("pe", pe_names), ("act", act_names), ("dve", dve_names), ("pool", pool_names)))
        XI = [Slot(sem(f"a_x{h}"), 1) for h in halves]
        KV = Slot(sem("a_kv"), 2)
        XO = Slot(sem("a_xo"), 2)
        s_t = [sem(f"a_ps{k}") for k in range(2)]
        blk = st.enter_context(nc.Block())

        def batch(d, i, h):
            v = d[i:i + 1] if isinstance(i, int) else d[bass.ds(i, 1)]
            return v.rearrange("o (n p) d -> p (o n) d", p=P)[:, h * TH:(h + 1) * TH, :]

        @blk.sync
        def _(e):
            for s in (PE, AC, DV, PO):
                e.sem_inc(s.sem, s.per)
            for s in (*XI, KV, XO):
                e.sem_inc(s.sem, 16 * s.per)
            with e.Fori(0, B) as i:
                for h in halves:
                    e.wait_ge(DV.sem, DV.done(i, ("rs", h, TH - 1), 1))
                    e.dma_start(xin[:, h * TH:(h + 1) * TH, :], batch(x, i, h)).then_inc(XI[h].sem, 16)
                e.wait_ge(PE.sem, PE.done(i, ("PV", 1, TH - 1), 1))
                e.wait_ge(AC.sem, AC.done(i, ("lt", 1, 1), 1))
                e.dma_start(kb[:], kr_dram[bass.ds(i, 1)].rearrange("o p k -> (o p) k")).then_inc(KV.sem, 16)
                e.dma_start(vw[:], vw_dram[bass.ds(i, 1)].rearrange("o p n d -> (o p) n d")).then_inc(KV.sem, 16)
                for h in halves:
                    e.wait_ge(DV.sem, DV.done(i, ("rs", h, TH - 1)))
                    e.dma_start(batch(x1_dram, i, h), xo[:]).then_inc(XO.sem, 16)
            e.wait_ge(XO.sem, XO.done(B - 1, 1))

        def pe_plan():
            for h in halves:
                for c in range(C):
                    def f(e, i, w, h=h, c=c):
                        w(AC, ("xh", h, TH - 1))
                        if c >= 2:
                            w(DV, ("lo", h, c - 2))
                        else:
                            w(DV, ("rs", h - 1 if h else 1, 2 + c), 0 if h else 1)
                        for t in range(TH):
                            last = e.transpose(ps[:, c % 2, t * P:(t + 1) * P], xh[:, t, c * P:(c + 1) * P], ident[:])
                        return last
                    yield ("T", h, c), f
                for n in range(H):
                    def f(e, i, w, h=h, n=n):
                        w(DV, ("qs", h, n - 2) if n >= 2 else ("lo", h, C - 1))
                        parts = [(a, b, c) for c in range(C) for a, b in ((qh, xTh), (qh, xTl), (ql, xTh))]
                        for k, (a, b, c) in enumerate(parts):
                            last = e.matmul(ps[:, 2 + n % 2, :], a[:, c, n * DH:(n + 1) * DH], b[:, c, :],
                                            start=(k == 0), stop=(k == len(parts) - 1))
                        return last
                    yield ("Q", h, n), f
                for p in range(2):
                    def f(e, i, w, h=h, p=p):
                        w(DV, ("qs", h, 2 * p + 1))
                        if p or h:
                            w(AC, ("lt", h if p else h - 1, 1 - p))
                        else:
                            w(AC, ("lt", 1, 1), 1)
                        e.wait_ge(KV.sem, KV.done(i, 1))
                        for k in range(2):
                            for n in range(2):
                                last = e.matmul(ps[n * S:(n + 1) * S, 4, :], kb[:, k * S:(k + 1) * S],
                                                (qc, qs)[k][:, 2 * p + n, :], start=(k == 0), stop=(k == 1))
                        return last
                    yield ("L", h, p), f
                for tp in range(2):
                    def f(e, i, w, h=h, tp=tp):
                        w(AC, ("lt", h, 1))
                        w(DV, ("sb", h - 1 if h else 1, tp), 0 if h else 1)
                        for t in range(2):
                            for p in range(2):
                                last = e.transpose(ps[:, 5 + tp, (2 * t + p) * P:(2 * t + p + 1) * P],
                                                   lt[:, p, (2 * tp + t) * P:(2 * tp + t + 1) * P], ident[:])
                        return last
                    yield ("LT", h, tp), f
                for tp in range(2):
                    def f(e, i, w, h=h, tp=tp):
                        w(PO, ("pr", h, tp))
                        if tp or h:
                            w(AC, ("pT", h if tp else h - 1, 1 - tp))
                        else:
                            w(AC, ("pT", 1, 1), 1)
                        for k in range(4):
                            last = e.transpose(ps[:, 7, k * P:(k + 1) * P], pr_[:, tp, k * P:(k + 1) * P], ident[:])
                        return last
                    yield ("PT", h, tp), f
                    for t in (2 * tp, 2 * tp + 1):
                        def f(e, i, w, h=h, tp=tp, t=t):
                            w(AC, ("pT", h, tp))
                            if t >= 2:
                                w(DV, ("rs", h, t - 2))
                            for p in range(2):
                                last = e.matmul(ps[:, t % 2, :], pT[:, tp, (2 * (t % 2) + p) * P:(2 * (t % 2) + p + 1) * P],
                                                vw[:, p, :], start=(p == 0), stop=(p == 1))
                            return last
                        yield ("PV", h, t), f

        @blk.tensor
        def _(e):
            run_steps(e, PE, list(pe_plan()), B)

        def act_plan():
            for h in halves:
                for t in range(TH):
                    def f(e, i, w, h=h, t=t):
                        w(PO, ("nb", h))
                        w(PE, ("T", h - 1 if h else 1, C - 1), 0 if h else 1)
                        return e.activation(xh[:, t, :], xin[:, h * TH + t, :], ACT.Identity,
                                            scale=sc[:, h, t:t + 1], bias=nb[:, h, t:t + 1])
                    yield ("xh", h, t), f
                for c in range(C):
                    def f(e, i, w, h=h, c=c):
                        w(PE, ("T", h, c))
                        w(PE, ("Q", h - 1 if h else 1, H - 1), 0 if h else 1)
                        return e.activation(xTh[:, c, :], ps[:, c % 2, :], ACT.Copy)
                    yield ("hi", h, c), f
                for p in range(2):
                    def f(e, i, w, h=h, p=p):
                        w(PE, ("L", h, p))
                        w(PE, ("LT", h - 1 if h else 1, 1), 0 if h else 1)
                        return e.activation(lt[:, p, :], ps[:, 4, :], ACT.Identity,
                                            scale=float(DH) ** -0.5, bias=kb[:, 2 * S:2 * S + 1])
                    yield ("lt", h, p), f
                for tp in range(2):
                    def f(e, i, w, h=h, tp=tp):
                        w(DV, ("sb", h, tp))
                        return e.activation(lg[:, tp, :], lg[:, tp, :], ACT.Exp)
                    yield ("ex", h, tp), f
                for tp in range(2):
                    def f(e, i, w, h=h, tp=tp):
                        w(PE, ("PT", h, tp))
                        w(PE, ("PV", h - 1 if h else 1, 2 * tp + 1), 0 if h else 1)
                        return e.activation(pT[:, tp, :], ps[:, 7, :], ACT.Copy)
                    yield ("pT", h, tp), f

        @blk.scalar
        def _(e):
            run_steps(e, AC, list(act_plan()), B)

        def heads(v):
            return v.rearrange("p (a s) -> p a s", s=S)

        def dve_plan():
            for h in halves:
                for t in range(TH):
                    def f(e, i, w, h=h, t=t):
                        e.wait_ge(XI[h].sem, XI[h].done(i))
                        return e.bn_stats(bst[:, h * TH + t, :], xin[:, h * TH + t, :])
                    yield ("st", h, t), f
                for t in range(TH):
                    def f(e, i, w, h=h, t=t):
                        if t == 0:
                            w(PO, ("nb", h), 1)
                            w(DV, ("st", h, TH - 1))
                            e.memset(junk[:], 0.0)
                        return e.bn_aggr(mv[:, h * TH + t, :], bst[:, h * TH + t, :])
                    yield ("ag", h, t), f
            for h in halves:
                for c in range(C):
                    def f(e, i, w, h=h, c=c):
                        w(AC, ("hi", h, c))
                        return e.tensor_tensor(xTl[:, c, :], ps[:, c % 2, :], xTh[:, c, :].bitcast(F32), ALU.subtract)
                    yield ("lo", h, c), f
                for n in range(H):
                    for o, tab, dst in (("qc", cos, qc), ("qs", sin, qs)):
                        def f(e, i, w, h=h, n=n, tab=tab, dst=dst):
                            w(PE, ("Q", h, n))
                            w(PE, ("L", h - 1 if h else 1, n // 2), 0 if h else 1)
                            return e.tensor_tensor(dst[:, n, :], ps[:, 2 + n % 2, :],
                                                   tab[:, S + h * HT:S + (h + 1) * HT], ALU.mult)
                        yield (o, h, n), f
                for tp in range(2):
                    def f(e, i, w, h=h, tp=tp):
                        w(PE, ("LT", h, tp))
                        return e.tensor_reduce(out=mx[:, tp, :], in_=heads(ps[:, 5 + tp, :]), op=ALU.max, axis=AX_X)
                    yield ("mx", h, tp), f
                for tp in range(2):
                    def f(e, i, w, h=h, tp=tp):
                        w(DV, ("mx", h, tp))
                        w(PO, ("pr", h - 1 if h else 1, tp), 0 if h else 1)
                        return e.tensor_tensor(heads(lg[:, tp, :]), heads(ps[:, 5 + tp, :]),
                                               mx[:, tp, :].unsqueeze(2).broadcast_to([P, 8, S]), ALU.subtract)
                    yield ("sb", h, tp), f
                for tp in range(2):
                    def f(e, i, w, h=h, tp=tp):
                        w(AC, ("ex", h, tp))
                        return e.tensor_reduce(out=sm[:, tp, :], in_=heads(lg[:, tp, :]), op=ALU.add, axis=AX_X)
                    yield ("sm", h, tp), f

                    def f(e, i, w, h=h, tp=tp):
                        w(DV, ("sm", h, tp))
                        return e.reciprocal(rc[:, tp, :], sm[:, tp, :])
                    yield ("rc", h, tp), f
                for t in range(TH):
                    def f(e, i, w, h=h, t=t):
                        w(PE, ("PV", h, t))
                        if t == 0:
                            e.wait_ge(XO.sem, XO.done(i, 0) if h else XO.done(i, 1, 1))
                        return e.tensor_tensor(xo[:, t, :], ps[:, t % 2, :], xin[:, h * TH + t, :], ALU.add)
                    yield ("rs", h, t), f

        @blk.vector
        def _(e):
            run_steps(e, DV, list(dve_plan()), B)

        def pool_plan():
            for h in halves:
                var, mean = mv[:, h * TH:(h + 1) * TH, 1], mv[:, h * TH:(h + 1) * TH, 0]
                nh = nhalf[:, 0:TH]
                chain = [
                    ("va", lambda e, v=var, h=h: e.tensor_tensor(va[:, h], v, eps_l[:, 0:TH], ALU.add)),
                    ("r1", lambda e, h=h, nh=nh: e.tensor_tensor(r1[:, h], va[:, h], nh, ALU.pow)),
                    ("vb", lambda e, v=var, h=h: e.tensor_tensor(vb[:, h], v, r1[:, h], ALU.mult)),
                    ("vc", lambda e, h=h: e.tensor_tensor(vc[:, h], vb[:, h], r1[:, h], ALU.mult)),
                    ("vd", lambda e, h=h: e.tensor_tensor(vb[:, h], vc[:, h], eps_r[:, 0:TH], ALU.add)),
                    ("r2", lambda e, h=h, nh=nh: e.tensor_tensor(r2[:, h], vb[:, h], nh, ALU.pow)),
                    ("sc", lambda e, h=h: e.tensor_tensor(sc[:, h], r1[:, h], r2[:, h], ALU.mult)),
                    ("ns", lambda e, h=h: e.tensor_tensor(vc[:, h], sc[:, h], none_[:, 0:TH], ALU.mult)),
                    ("nb", lambda e, m=mean, h=h: e.tensor_tensor(nb[:, h], m, vc[:, h], ALU.mult)),
                ]
                for k, (o, g) in enumerate(chain):
                    def f(e, i, w, h=h, k=k, g=g, chain=chain):
                        if k == 0:
                            w(DV, ("ag", h, TH - 1))
                            w(AC, ("xh", h, TH - 1), 1)
                        else:
                            w(PO, (chain[k - 1][0], h))
                        return g(e)
                    yield (o, h), f
            for h in halves:
                for tp in range(2):
                    def f(e, i, w, h=h, tp=tp):
                        w(DV, ("rc", h, tp))
                        w(PE, ("PT", h - 1 if h else 1, tp), 0 if h else 1)
                        return e.tensor_tensor(heads(pr_[:, tp, :]), heads(lg[:, tp, :]),
                                               rc[:, tp, :].unsqueeze(2).broadcast_to([P, 8, S]), ALU.mult)
                    yield ("pr", h, tp), f

        @blk.gpsimd
        def _(e):
            run_steps(e, PO, list(pool_plan()), B)


def experts(nc, sem, ps, w1, ident, small, gate_f, s_w1, Wc, bc, b1, b2, tie_in, gmask_in,
            x1_dram, w2_dram, out):
    nhalf, none_, eps_l, eps_r = small
    st = ExitStack()
    with st:
        sb = lambda n, s, dt=F32: st.enter_context(nc.sbuf_tensor(n, s, dt))
        NP_ = NT // 2
        QH = Q // 2
        GB = NP_
        wc = sb("wc", [P, C, E])
        bcol = sb("bcol", [P, 1])
        b1c = sb("b1c", [P, Q])
        b2s = sb("b2s", [P, D])
        tie = sb("tie", [P, G])
        gmask = sb("gmask", [P, GT])
        w2s = sb("w2s", [P, 4, QB * P])
        xin = sb("b_xin", [P, 4, D])
        xf = sb("xf", [P, 2, D])
        xnh = sb("xnh", [P, NT, D], F32R)
        xnl = sb("xnl", [P, NT, D], F32R)
        gat = sb("gat", [P, 2, QH * 4 * NG])
        xT = gat[:].rearrange("p h (c t) -> p h c t", t=HT)
        lgt = sb("lgt", [P, HT])
        top_ = sb("top", [P, HT // G])
        selT = sb("selT", [P, T])
        sel = sb("sel", [P, NT, P], BF16)
        selb = sb("selb", [P, NT, QH * 4 * GT], F32R)
        hid = sb("hid", [P, Q, 4 * NG])
        hb = lgt
        res = sb("res", [P, 2, Q * P])
        y = sb("y", [P, 2, 4, P])
        bst = sb("b_bst", [P, NT, 6])
        junk = sb("b_junk", [P, 1])
        mv = sb("b_mv", [P, NT, 2])
        va = sb("b_va", [P, NP_, 2])
        r1 = sb("b_r1", [P, NP_, 2])
        ns = sb("b_ns", [P, NP_, 2])
        nb = sb("b_nb", [P, NP_, 2])

        halves = range(2)

        def pe_names():
            for t in range(NT):
                yield ("T", t)
                if t % TH == TH - 1:
                    yield ("lg", t // TH)
            yield from (("sT", h) for h in halves)
            prev = None
            for eh in halves:
                for c in range(C):
                    yield from (("ga", eh, c, k) for k in range(GB))
                    if prev:
                        yield ("w1",) + prev
                    prev = (eh, c)
            yield ("w1",) + prev
            for c in range(C):
                yield from (("w2", c, b) for b in range(Q // QB))
                if c:
                    yield from (("sc", c - 1, h) for h in halves)
            yield from (("sc", C - 1, h) for h in halves)

        def act_names():
            for t in range(NT):
                yield ("xf", t)
                yield ("hi", t)
                yield ("xT", t)
            yield from (("sel", h) for h in halves)
            for eh in halves:
                for c in range(C):
                    yield from (("ga", eh, c, k) for k in range(0, GB, 2))
            for c in range(C):
                yield from (("rs", c, b) for b in range(Q // QB))

        def dve_names():
            for t in range(NT):
                yield ("st", t)
                if t % 2:
                    yield ("ag", t - 1)
                    yield ("ag", t)
            for h in halves:
                yield ("lg", h)
                yield ("mx", h)
                yield ("eq", h)
            for eh in halves:
                for c in range(C):
                    yield from (("ga", eh, c, k) for k in range(1, GB, 2))
                    if c == C - 1:
                        for b in range(4):
                            yield ("hb", eh, b)
                            yield ("hr", eh, b)
            for c in range(C):
                yield ("tr", c)
                yield from (("fin", c, h) for h in halves)

        def pool_names():
            for k in range(NP_):
                yield from ((o, k) for o in ("va", "r1", "ns", "nb"))
                yield from (("lo", t) for t in (2 * k, 2 * k + 1))
            yield from (("sp", eh, t) for eh in halves for t in range(NT))

        PE, AC, DV, PO = (Steps(sem(f"b_{n}s"), list(l())) for n, l in
                          (("pe", pe_names), ("act", act_names), ("dve", dve_names), ("pool", pool_names)))
        XI = [Slot(sem(f"b_x{k}"), NT // 4) for k in range(4)]
        W2S = [Slot(sem(f"b_w2{k}"), 2 * C) for k in range(4)]
        YL = [Slot(sem(f"b_yl{k}"), C) for k in range(2)]
        YS = [Slot(sem(f"b_ys{k}"), C) for k in range(2)]
        s_c = sem("b_const")
        consts = [(wc[:], Wc.rearrange("(c p) e s -> p c (e s)", p=P)), (bcol[:], bc),
                  (b2s[:], b2.rearrange("e s d -> (e s) d")), (tie[:], tie_in.partition_broadcast(P)),
                  (gmask[:], gmask_in), (b1c[:], b1)]
        s_m = sem("b_zero")
        blk = st.enter_context(nc.Block())

        def batch(d, i, t0, n):
            return d[bass.ds(i, 1)].rearrange("o (n p) d -> p (o n) d", p=P)[:, t0:t0 + n, :]

        def store(e, i, c, h):
            e.wait_ge(DV.sem, DV.done(i, ("fin", c, h)))
            e.dma_start(batch(out, i, h * TH, TH)[:, :, c * P:(c + 1) * P], y[:, h]).then_inc(YS[h].sem, 16)

        @blk.sync
        def _(e):
            for s in (PE, AC, DV, PO):
                e.sem_inc(s.sem, s.per)
            for s in (*XI, *W2S, *YL, *YS):
                e.sem_inc(s.sem, 16 * s.per)
            for o, s in consts:
                e.dma_start(o, s).then_inc(s_c, 16)
            with e.Fori(0, B) as i:
                for t in range(NT):
                    u = (t - 4) % NT
                    e.wait_ge(AC.sem, AC.done(i, ("hi", u), t < 4))
                    e.dma_start(xin[:, t % 4, :], batch(x1_dram, i, t, 1)[:, 0]).then_inc(XI[t % 4].sem, 16)
                for c in range(C):
                    for b in range(Q // QB):
                        n = (8 * c + b - 4) % (8 * C)
                        e.wait_ge(PE.sem, PE.done(i, ("w2", n // 8, n % 8), c == 0 and b < 4))
                        e.dma_start(w2s[:, b % 4, :], w2_dram[c, b]).then_inc(W2S[b % 4].sem, 16)
                    for h in halves:
                        if c:
                            store(e, i, c - 1, h)
                        e.wait_ge(YS[h].sem, YS[h].done(i, (c - 1) % C, c == 0))
                        e.dma_start(y[:, h], batch(x1_dram, i, h * TH, TH)[:, :, c * P:(c + 1) * P]).then_inc(YL[h].sem, 16)
                for h in halves:
                    store(e, i, C - 1, h)
            for h in halves:
                e.wait_ge(YS[h].sem, YS[h].done(B - 1, C - 1))

        def pe_plan():
            acts = {}
            for t in range(NT):
                def f(e, i, w, t=t):
                    w(AC, ("xf", t))
                    w(AC, ("xT", (t - 2) % NT), t < 2)
                    if t < 2:
                        w(DV, ("fin", C - 1, 1), 1)
                    for c in range(C):
                        last = e.transpose(ps[:, 2 + t % 2, c * P:(c + 1) * P], xf[:, t % 2, c * P:(c + 1) * P], ident[:])
                    return last
                acts[("T", t)] = f
            for h in halves:
                def f(e, i, w, h=h):
                    w(AC, ("xT", h * TH + TH - 1))
                    e.wait_ge(s_c, 16 * len(consts))
                    w(DV, ("lg", 0)) if h else w(AC, ("rs", C - 1, 7), 1)
                    for c in range(C):
                        last = e.matmul(ps[:, 4, :], wc[:, c, :], xT[:, h, c, :], start=(c == 0), stop=(c == C - 1))
                    return last
                acts[("lg", h)] = f

                def f(e, i, w, h=h):
                    w(DV, ("eq", h))
                    w(AC, ("rs", C - 1, 7), 1)
                    for t in range(TH):
                        last = e.transpose(ps[:, 5 + h, t * P:(t + 1) * P], selT[:, (h * TH + t) * P:(h * TH + t + 1) * P], ident[:])
                    return last
                acts[("sT", h)] = f
            for eh in halves:
                for c in range(C):
                    for k in range(GB):
                        def f(e, i, w, eh=eh, c=c, k=k):
                            w(PO, ("sp", eh, 2 * k + 1))
                            if eh == 0 and c == 0:
                                w(AC, ("sel", 1)); w(DV, ("lg", 1))
                            else:
                                pe, pc = (eh, c - 1) if c else (eh - 1, C - 1)
                                w(DV if k % 2 else AC, ("ga", pe, pc, k))
                            for t in range(2):
                                for m, part in enumerate((xnh, xnl)):
                                    last = e.matmul(ps[:, 4 + k, t * 256:(t + 1) * 256], part[:, 2 * k + t, c * P:(c + 1) * P],
                                                    selb[:, 2 * k + t, :], start=(m == 0), stop=(m == 1))
                            return last
                        acts[("ga", eh, c, k)] = f

                    def f(e, i, w, eh=eh, c=c):
                        e.wait_ge(s_w1, 16)
                        w(AC, ("ga", eh, c, GB - 2)); w(DV, ("ga", eh, c, GB - 1))
                        if eh == 0 and c == 0:
                            w(DV, ("fin", C - 1, 1), 1); w(AC, ("xT", NT - 1))
                        for q in range(QH):
                            if c == 0 and q % QB == 0 and eh:
                                w(DV, ("hb", 0, q // QB))
                            wv = w1[:, c, (eh * QH + q) * P:(eh * QH + q + 1) * P]
                            last = e.matmul(ps[:, q // QB, (q % QB) * P:(q % QB + 1) * P], wv,
                                            gat[:, c % 2, q * P:(q + 1) * P],
                                            start=(c == 0 and q % QB == 0), stop=(c == C - 1), skip_group_check=True)
                        return last
                    acts[("w1", eh, c)] = f
            for c in range(C):
                for b in range(Q // QB):
                    def f(e, i, w, c=c, b=b):
                        if c == 0 and b == 0:
                            w(AC, ("ga", 1, C - 1, GB - 2)); w(DV, ("ga", 1, C - 1, GB - 1))
                        w(DV, ("hr", b // 4, b % 4))
                        e.wait_ge(W2S[b % 4].sem, W2S[b % 4].done(i, 2 * c + b // 4))
                        if c or b >= 4:
                            n = c * 8 + b - 4
                            w(AC, ("rs", n // 8, n % 8))
                        for j in range(QB):
                            q = QB * b + j
                            last = e.matmul(ps[:, 4 + b % 4, j * P:(j + 1) * P], hid[:, q, :],
                                            w2s[:, b % 4, j * P:(j + 1) * P], start=True, stop=True)
                        return last
                    acts[("w2", c, b)] = f
                for h in halves:
                    def f(e, i, w, c=c, h=h):
                        w(DV, ("tr", c))
                        if c:
                            w(DV, ("fin", c - 1, h))
                        r = res[:, c % 2, :].rearrange("p (g d) -> p g d", d=P)
                        for t in range(TH):
                            tt = h * TH + t
                            e.matmul(ps[:, h, t * P:(t + 1) * P], selT[:, tt * P:(tt + 1) * P], b2s[:, c * P:(c + 1) * P],
                                     start=(t == 0), stop=False, skip_group_check=True)
                            for g in range(GT):
                                last = e.matmul(ps[g * G:(g + 1) * G, h, t * P:(t + 1) * P],
                                                selT[:, tt * P + g * G:tt * P + (g + 1) * G], r[:, tt * GT + g, :],
                                                start=False, stop=(t == TH - 1 and g == GT - 1), skip_group_check=True)
                        return last
                    acts[("sc", c, h)] = f
            return [(n, acts[n]) for n in pe_names()]

        @blk.tensor
        def _(e):
            run_steps(e, PE, pe_plan(), B)

        def gather_copy(e, w, eh, c, k, copy):
            w(PE, ("ga", eh, c, k))
            if c >= 2:
                w(PE, ("w1", eh, c - 2))
            elif eh:
                w(PE, ("w1", 0, c + 2))
            else:
                w(PE, ("lg", c))
            dst = gat[:, c % 2, :].rearrange("p (qj t g) -> p t qj g", t=NT, g=GT)[:, 2 * k:2 * k + 2]
            return copy(dst, ps[:, 4 + k, :].rearrange("p (t qj g) -> p t qj g", t=2, g=GT))

        def act_plan():
            acts = {}
            for t in range(NT):
                def f(e, i, w, t=t):
                    w(PO, ("nb", t // 2))
                    w(PE, ("T", (t - 2) % NT), t < 2)
                    w(PO, ("lo", (t - 2) % NT), t < 2)
                    return e.activation(xf[:, t % 2, :], xin[:, t % 4, :], ACT.Identity,
                                        scale=r1[:, t // 2, t % 2:t % 2 + 1], bias=nb[:, t // 2, t % 2:t % 2 + 1])
                acts[("xf", t)] = f

                def f(e, i, w, t=t):
                    w(PE, ("ga", 1, C - 1, GB - 1), 1)
                    return e.activation(xnh[:, t, :], xin[:, t % 4, :], ACT.Identity,
                                        scale=r1[:, t // 2, t % 2:t % 2 + 1], bias=nb[:, t // 2, t % 2:t % 2 + 1])
                acts[("hi", t)] = f

                def f(e, i, w, t=t):
                    w(PE, ("T", t))
                    w(PE, ("w1", 1, C - 1), 1)
                    return e.activation(xT[:, t // TH, :, (t % TH) * P:(t % TH + 1) * P],
                                        ps[:, 2 + t % 2, :].rearrange("p (c t) -> p c t", t=P), ACT.Copy)
                acts[("xT", t)] = f
            for h in halves:
                def f(e, i, w, h=h):
                    w(PE, ("sT", h))
                    w(PO, ("sp", 1, NT - 1), 1)
                    return e.activation(sel[:, h * TH:(h + 1) * TH, :].rearrange("p t e -> p (t e)"), ps[:, 5 + h, :], ACT.Copy)
                acts[("sel", h)] = f
            for eh in halves:
                for c in range(C):
                    for k in range(0, GB, 2):
                        acts[("ga", eh, c, k)] = lambda e, i, w, eh=eh, c=c, k=k: gather_copy(
                            e, w, eh, c, k, lambda o, v: e.activation(o, v, ACT.Copy))
            for c in range(C):
                for b in range(Q // QB):
                    def f(e, i, w, c=c, b=b):
                        w(PE, ("w2", c, b))
                        w(PE, ("sc", (c - 2) % C, 1), c < 2)
                        return e.activation(res[:, c % 2, b * 512:(b + 1) * 512], ps[:, 4 + b % 4, :], ACT.Copy)
                    acts[("rs", c, b)] = f
            return [(n, acts[n]) for n in act_names()]

        @blk.scalar
        def _(e):
            run_steps(e, AC, act_plan(), B)

        def dve_plan():
            acts = {}
            for t in range(NT):
                def f(e, i, w, t=t):
                    e.wait_ge(XI[t % 4].sem, XI[t % 4].done(i, t // 4))
                    return e.bn_stats(bst[:, t, :], xin[:, t % 4, :])
                acts[("st", t)] = f

                def f(e, i, w, t=t):
                    if t % 2 == 0:
                        w(PO, ("nb", t // 2), 1)
                        w(DV, ("st", t + 1))
                        e.memset(junk[:], 0.0)
                    return e.bn_aggr(mv[:, t, :], bst[:, t, :])
                acts[("ag", t)] = f
            for h in halves:
                def f(e, i, w, h=h):
                    w(PE, ("lg", h))
                    w(DV, ("eq", 0) if h else ("eq", 1), 0 if h else 1)
                    v = lambda a: a.rearrange("p (n t) -> p n t", t=G)
                    return e.scalar_tensor_tensor(out=v(lgt[:]), in0=v(ps[:, 4, :]), scalar=bcol[:],
                                                  in1=tie[:].unsqueeze(1).broadcast_to([P, HT // G, G]), op0=ALU.add, op1=ALU.add)
                acts[("lg", h)] = f

                def f(e, i, w, h=h):
                    w(DV, ("lg", h))
                    return e.tensor_reduce(out=top_[:], in_=lgt[:].rearrange("p (n t) -> p n t", t=G), op=ALU.max, axis=AX_X)
                acts[("mx", h)] = f

                def f(e, i, w, h=h):
                    w(DV, ("mx", h))
                    w(PE, ("sc", C - 1, 1), 1)
                    return e.tensor_tensor(selT[:, h * HT:(h + 1) * HT].rearrange("p (n t) -> p n t", t=G),
                                           lgt[:].rearrange("p (n t) -> p n t", t=G),
                                           top_[:].unsqueeze(2).broadcast_to([P, HT // G, G]), ALU.is_equal)
                acts[("eq", h)] = f
            for eh in halves:
                for c in range(C):
                    for k in range(1, GB, 2):
                        acts[("ga", eh, c, k)] = lambda e, i, w, eh=eh, c=c, k=k: gather_copy(
                            e, w, eh, c, k, lambda o, v: e.tensor_copy(o, v))
                for b in range(4):
                    q0 = eh * QH + b * QB

                    def f(e, i, w, eh=eh, b=b, q0=q0):
                        w(PE, ("w1", eh, C - 1))
                        if b or eh:
                            w(DV, ("hr", eh if b else eh - 1, (b - 1) % 4))
                        else:
                            w(DV, ("hr", 1, 3), 1)
                        return e.tensor_tensor(hb[:].rearrange("p (q n) -> p q n", n=P), ps[:, b, :].rearrange("p (q n) -> p q n", n=P),
                                               b1c[:, q0:q0 + QB].unsqueeze(2).broadcast_to([P, QB, P]), ALU.add)
                    acts[("hb", eh, b)] = f

                    def f(e, i, w, eh=eh, b=b, q0=q0):
                        w(DV, ("hb", eh, b))
                        w(PE, ("w2", C - 1, Q // QB - 1), 1)
                        last = None
                        for j in range(4):
                            last = e.tensor_scalar(hid[j * F:(j + 1) * F, q0:q0 + QB, j * NG:(j + 1) * NG],
                                                   hb[j * F:(j + 1) * F, :].rearrange("p (q n) -> p q n", n=P)[:, :, j * NG:(j + 1) * NG],
                                                   0.0, None, ALU.max)
                        return last
                    acts[("hr", eh, b)] = f
            for c in range(C):
                def f(e, i, w, c=c):
                    w(AC, ("rs", c, Q // QB - 1))
                    v = res[:, c % 2, :].rearrange("p (q d) -> p d q", d=P)
                    return e.transpose(v, v)
                acts[("tr", c)] = f
                for h in halves:
                    def f(e, i, w, c=c, h=h):
                        w(PE, ("sc", c, h))
                        e.wait_ge(YL[h].sem, YL[h].done(i, c))
                        v = y[:, h].rearrange("p t d -> p (t d)")
                        return e.scalar_tensor_tensor(out=v, in0=ps[:, h, :], scalar=gate_f[:], in1=v, op0=ALU.mult, op1=ALU.add)
                    acts[("fin", c, h)] = f
            return [(n, acts[n]) for n in dve_names()]

        @blk.vector
        def _(e):
            e.memset(hid[:], 0.0).then_inc(s_m, 1)
            e.wait_ge(s_m, 1)
            e.wait_ge(s_c, 16 * len(consts))
            run_steps(e, DV, dve_plan(), B)

        def pool_plan():
            acts = {}
            for k in range(NP_):
                var, mean = mv[:, 2 * k:2 * k + 2, 1], mv[:, 2 * k:2 * k + 2, 0]

                def f(e, i, w, k=k, v=var):
                    w(DV, ("ag", 2 * k + 1))
                    return e.tensor_tensor(va[:, k], v, eps_l[:, 0:2], ALU.add)
                acts[("va", k)] = f

                def f(e, i, w, k=k):
                    w(PO, ("va", k)); w(AC, ("hi", 2 * k + 1), 1)
                    return e.tensor_tensor(r1[:, k], va[:, k], nhalf[:, 0:2], ALU.pow)
                acts[("r1", k)] = f

                def f(e, i, w, k=k):
                    w(PO, ("r1", k))
                    return e.tensor_tensor(ns[:, k], r1[:, k], none_[:, 0:2], ALU.mult)
                acts[("ns", k)] = f

                def f(e, i, w, k=k, m=mean):
                    w(PO, ("ns", k))
                    return e.tensor_tensor(nb[:, k], m, ns[:, k], ALU.mult)
                acts[("nb", k)] = f
                for t in (2 * k, 2 * k + 1):
                    def f(e, i, w, t=t):
                        w(AC, ("hi", t))
                        w(PE, ("ga", 1, C - 1, GB - 1), 1)
                        return e.tensor_tensor(xnl[:, t, :], xf[:, t % 2, :], xnh[:, t, :].bitcast(F32), ALU.subtract)
                    acts[("lo", t)] = f
            for eh in halves:
                for t in range(NT):
                    def f(e, i, w, eh=eh, t=t):
                        e.wait_ge(s_c, 16 * len(consts))
                        w(AC, ("sel", t // TH))
                        w(PE, ("ga", 0, C - 1, t // 2) if eh else ("ga", 1, C - 1, t // 2), 0 if eh else 1)
                        s = sel[:, t, :].rearrange("p (j q) -> p q j", q=Q)[:, eh * QH:(eh + 1) * QH, :]
                        return e.tensor_tensor(selb[:, t, :].rearrange("p (q j g) -> p q j g", j=4, g=GT),
                                               s.unsqueeze(3).broadcast_to([P, QH, 4, GT]),
                                               gmask[:].unsqueeze(1).unsqueeze(1).broadcast_to([P, QH, 4, GT]), ALU.mult)
                    acts[("sp", eh, t)] = f
            return [(n, acts[n]) for n in pool_names()]

        @blk.gpsimd
        def _(e):
            run_steps(e, PO, pool_plan(), B)


def kernel(x, ctx_1024, mask_BxS2_bk0, g_xattn, g_ffn, L0_xattn_rms_scale, L0_xattn_q_w, L0_xattn_kv_w,
           L0_xattn_out_w, L0_ffn_Wc, L0_ffn_bc, L0_ffn_W1, L0_ffn_b1, L0_ffn_W2, L0_ffn_b2):
    from concourse import bacc
    from concourse.bass_utils import run_bass_kernel_spmd

    half = np.arange(DH // 2, dtype=np.float32)
    scale = np.float32(10000.0) ** (np.float32(2.0 / DH) * half)
    angle = np.arange(S + T, dtype=np.float32)[None, :] / scale[:, None]
    cos = np.concatenate([np.cos(angle), np.cos(angle)]).astype(np.float32)
    sin = np.concatenate([np.sin(angle), -np.sin(angle)]).astype(np.float32)
    tie = np.linspace(0.0, 1e-6, G, dtype=np.float32)
    gmask = np.repeat(np.eye(GT, dtype=np.float32), G, axis=0)

    w1 = np.asarray(L0_ffn_W1).reshape(4, Q, C, P, F).transpose(3, 2, 1, 0, 4).reshape(P, C, E * F)
    w2 = np.asarray(L0_ffn_W2).reshape(4, Q // QB, QB, C, P, F).transpose(3, 1, 0, 5, 2, 4).reshape(C, Q // QB, P, QB * P)
    b1 = np.asarray(L0_ffn_b1).reshape(4, Q, F).transpose(0, 2, 1).reshape(P, Q)

    arrays = {
        "x": x, "ctx_1024": ctx_1024, "mask": np.asarray(mask_BxS2_bk0).T, "g_xattn": g_xattn, "g_ffn": g_ffn,
        "rms": np.asarray(L0_xattn_rms_scale).reshape(C, P).T, "q_w": L0_xattn_q_w, "kv_w": L0_xattn_kv_w, "out_w": L0_xattn_out_w,
        "Wc": L0_ffn_Wc, "bc": np.asarray(L0_ffn_bc).reshape(E, 1), "W1": w1, "b1": b1, "W2": w2, "b2": L0_ffn_b2,
        "ident": np.eye(P, dtype=np.float32), "cos": cos, "sin": sin, "tie": tie, "gmask": gmask,
    }
    arrays = {n: np.ascontiguousarray(a) for n, a in arrays.items()}
    nc = bacc.Bacc("TRN2", target_bir_lowering=False, num_devices=1)
    args = [nc.dram_tensor(f"in_{n}", a.shape, mybir.dt.from_np(a.dtype), kind="ExternalInput").ap() for n, a in arrays.items()]
    out = nc.dram_tensor("out", (B, T, D), F32, kind="ExternalOutput").ap()
    build(nc, *args, out)
    r = run_bass_kernel_spmd(nc, [{f"in_{n}": a for n, a in arrays.items()}], core_ids=[0])
    return r.results[0]["out"]
```

```python
from contextlib import ExitStack

import numpy as np

import concourse.bass as bass
from concourse import mybir
from concourse.alu_op_type import AluOpType as ALU

F32 = mybir.dt.float32
F32R = mybir.dt.float32r
BF16 = mybir.dt.bfloat16
U8 = mybir.dt.uint8
ACT = mybir.ActivationFunctionType
AX_X = mybir.AxisListType.X

P = 128
B, T, D = 16, 1024, 512
S = 64
H, DH = 4, 128
E, G = 128, 32
F = 32
C = D // P
NT = T // P
TH = NT // 2
HT = T // 2
GT = P // G
NG = T // G
Q = E // 4
QB = 4
FILL = -2.3819763e38
LN_EPS, RMS_EPS = 1e-5, 1e-6


class Steps:

    def __init__(self, sem, names, unit=1):
        self.sem, self.per, self.unit = sem, len(names), unit
        self.place = {n: k + 1 for k, n in enumerate(names)}
        assert len(self.place) == self.per

    def done(self, i, name, back=0):
        return i * (self.unit * self.per) + self.unit * ((1 - back) * self.per + self.place[name])


def run_steps(eng, steps, plan):
    for name, fn in plan:
        seen = {}

        def wait(who, what, back=0):
            at = who.done(0, what, back)
            if id(who) in seen:
                assert at <= seen[id(who)], (name, what)
                return
            seen[id(who)] = at
            eng.wait_ge(who.sem, at)
        fn(eng, 0, wait).then_inc(steps.sem, 1)


class Phase:

    def __init__(self, nc, sem, label, plans, slots, lead, rounds):
        self.nc, self.plans, self.slots, self.lead = nc, plans, slots, lead
        self.slot_of = {n: k for k, names in slots.items() for n in names}
        for kind, keep, over in (("first", lead, (-1,)), ("loop", lambda n: True, (0, rounds - 1)),
                                 ("last", lambda n: not lead(n), (rounds - 1,))):
            self.block(sem, label + kind, kind, keep, over)

    def block(self, sem, label, kind, keep, over):
        tracks = {}
        for k, plan in self.plans.items():
            if k != "sync":
                tracks[k] = Steps(sem(f"{label}_{k}"), [n for n, _ in plan if keep(n)])
        for k, names in self.slots.items():
            tracks[k] = Steps(sem(f"{label}_{k}"), [n for n in names if keep(n)], unit=16)

        def emit(eng, key, i):
            for name, fn in self.plans[key]:
                if not keep(name):
                    continue
                seen = {}
                ahead = int(self.lead(name))

                def wait(who, what, ago=0):
                    back = ago + int(self.lead(what)) - ahead
                    if kind != "loop" and (back or what not in tracks[who].place):
                        assert back >= 0
                        return
                    if back >= 2:
                        raise AssertionError((name, what, "too old"))
                    assert back >= 0, (name, what, "is in the future")
                    at = tracks[who].done(0, what, back)
                    if who in seen:
                        assert at <= seen[who], (name, who, what)
                        return
                    seen[who] = at
                    base = i if kind == "loop" else -1
                    eng.wait_ge(tracks[who].sem, tracks[who].done(base, what, back))
                last = fn(eng, i + ahead, wait)
                t = tracks[self.slot_of[name] if key == "sync" else key]
                last.then_inc(t.sem, t.unit)

        def program(key, eng):
            if key == "sync":
                if kind == "loop":
                    for t in tracks.values():
                        eng.sem_inc(t.sem, t.unit * t.per)
            if kind == "loop":
                with eng.Fori(*over) as i:
                    emit(eng, key, i)
            else:
                emit(eng, key, over[0])
            if key == "sync":
                for k in self.slots:
                    n = tracks[k].per
                    if n:
                        eng.wait_ge(tracks[k].sem, 16 * n * (over[1] + 1 if kind == "loop" else 1))

        with self.nc.Block() as blk:
            blk.sync(lambda e: program("sync", e))
            blk.gpsimd(lambda e: program("pool", e))
            blk.scalar(lambda e: program("act", e))
            blk.vector(lambda e: program("dve", e))
            blk.tensor(lambda e: program("pe", e))


def build(nc, x, ctx_in, mask, gx_in, gf_in, rms, q_w, kv_w, out_w, Wc, bc, W1, b1, W2, b2,
          ident_in, cos_in, sin_in, tie_in, gmask_in, out):
    x1_dram = nc.dram_tensor("x1_scratch", (B, T, D), F32, kind="Internal").ap()
    kr_dram = nc.dram_tensor("k_scratch", (B, P, 2 * S + 1), F32, kind="Internal").ap()
    vw_dram = nc.dram_tensor("vw_scratch", (B, P, 2, 2, D), F32, kind="Internal").ap()

    top = ExitStack()

    def sem(name):
        return top.enter_context(nc.semaphore(name))

    with top:
        ps = top.enter_context(nc.psum_tensor("ps", [P, 8, 512], F32))
        sb0 = lambda n, s, dt=F32: top.enter_context(nc.sbuf_tensor(n, s, dt))
        w1 = sb0("w1", [P, C, E * F])
        ident = sb0("ident", [P, P])
        nhalf = sb0("nhalf", [P, 8])
        none_ = sb0("neg_one", [P, 8])
        eps_l = sb0("eps_layer", [P, 8])
        eps_r = sb0("eps_rms", [P, 8])
        small = (nhalf, none_, eps_l, eps_r)
        gate_x = sb0("gate_x", [P, 1])
        gate_f = sb0("gate_f", [P, 1])
        s_w1 = sem("s_w1")
        attn = ExitStack()
        with attn:
            sba = lambda n, s, dt=F32: attn.enter_context(nc.sbuf_tensor(n, s, dt))
            cos = sba("cos", [P, S + T])
            sin = sba("sin", [P, S + T])
            qh = sba("qh", [P, C, D], F32R)
            ql = sba("ql", [P, C, D], F32R)
            prologue(nc, sem, ps, w1, ident, small, gate_x, gate_f, cos, sin, qh, ql, s_w1,
                     ctx_in, mask, gx_in, gf_in, rms, q_w, kv_w, out_w, W1,
                     ident_in, cos_in, sin_in, kr_dram, vw_dram)
            attention(nc, sem, ps, ident, small, cos, sin, qh, ql, x, kr_dram, vw_dram, x1_dram)
        experts(nc, sem, ps, w1, ident, small, gate_f, s_w1, Wc, bc, b1, b2, tie_in, gmask_in,
                x1_dram, W2, out)


def prologue(nc, sem, ps, w1, ident, small, gate_x, gate_f, cos, sin, qh, ql, s_w1,
             ctx_in, mask, gx_in, gf_in, rms, q_w, kv_w, out_w, W1,
             ident_in, cos_in, sin_in, kr_dram, vw_dram):
    nhalf, none_, eps_l, eps_r = small
    st = ExitStack()
    with st:
        sb = lambda n, s, dt=F32: st.enter_context(nc.sbuf_tensor(n, s, dt))
        NC = B * S // P
        cx = sb("cx", [P, NC, D])
        mnT = sb("mnT", [P, C, B * S])
        vT = sb("vT", [P, B * S])
        kr = sb("kr", [P, B, 2 * S + 1])
        kt = sb("kt", [P, 2, HT])
        ow = sb("ow", [P, H, D])
        qraw = sb("qraw", [P, C, H, DH])
        kvraw = sb("kvraw", [P, C, 2 * DH])
        kvs = sb("kvs", [P, C, 3 * DH])
        vwb = sb("vwb", [P, 2, 2, 2, D], F32R)
        rs1 = sb("rs1", [P, C])
        mk = sb("mk", [P, B], U8)
        mkf = sb("mkf", [P, B])
        bst = sb("bst", [P, NC, 6])
        mv = sb("mv", [P, NC, 2])
        ms = sb("ms", [P, NC])
        ms2 = sb("ms2", [P, NC])
        rr = sb("rr", [P, NC])
        gts = sb("gts", [P, 2])

        names = ["ctx", "small", "qw", "kvw", "ow", "tab"]
        L = {n: sem(f"p_{n}") for n in names}
        s_vws = [sem(f"p_vws{k}") for k in range(2)]
        s_krs = sem("p_krs")
        count = {}

        cT = [("cT", c, h) for c in range(C) for h in range(2)]
        kj = [("k", w, h) for w in range(2) for h in range(2)]
        vj = [("v", h) for h in range(2)]
        vwj = [("vw", b, pr) for b in range(B) for pr in range(2)]
        pe_names = cT + kj + vj + vwj
        act_names = (["gate"] + [("cn", t) for t in range(NC)] + [("mn",) + n[1:] for n in cT]
                     + [("vT", h) for h in range(2)] + [("vwe", b, pr) for b in range(B) for pr in range(2)])
        rope = [(o, h) for h in range(2) for o in ("kC", "sS", "k0", "sC", "kS", "k1")]
        dve_names = (["sc1"] + [("st", t) for t in range(NC)] + [("ag", t) for t in range(NC)]
                     + [("qs", c) for c in range(C)] + ["qhi", "qlo"]
                     + [("kvs", c) for c in range(C)] + [("ks1", c) for c in range(C)] + [("ks2", c) for c in range(C)]
                     + ["mkf", "mkb"] + rope + [("vwl", b, pr) for b in range(B) for pr in range(2)])
        pool_names = ["nh", "ms0", "ms1", "ms2", "ms3"]
        PE, AC, DV, PO = (Steps(sem(f"p_{n}s"), l) for n, l in
                          (("pe", pe_names), ("act", act_names), ("dve", dve_names), ("pool", pool_names)))

        blk = st.enter_context(nc.Block())

        @blk.sync
        def _(e):
            def load(name, *pairs):
                for o, s in pairs:
                    e.dma_start(o, s).then_inc(L[name], 16)
                    count[name] = count.get(name, 0) + 16
            for s in (PE, AC, DV, PO):
                e.sem_inc(s.sem, s.per)
            load("small", (rs1[:], rms),
                 (gts[:, 0:1], gx_in.partition_broadcast(P)), (gts[:, 1:2], gf_in.partition_broadcast(P)),
                 (mk[0:S, :], mask), (mk[S:P, :], mask),
                 (ident[:], ident_in))
            load("ctx", (cx[:], ctx_in.rearrange("b s d -> (b s) d").rearrange("(n p) d -> p n d", p=P)))
            load("kvw", *[(kvraw[:, :, k * DH:(k + 1) * DH], kv_w[k, 0].rearrange("(c p) h -> p c h", p=P)) for k in range(2)])
            load("qw", *[(qraw[:, :, n, :], q_w[n].rearrange("(c p) h -> p c h", p=P)) for n in range(H)])
            load("tab", (cos[:], cos_in), (sin[:], sin_in))
            load("ow", (ow[:], out_w.rearrange("n h d -> h n d")))

            def store_vw(b):
                e.wait_ge(DV.sem, DV.done(0, ("vwl", b, 1)))
                e.dma_start(vw_dram[b], vwb[:, b % 2].bitcast(F32)).then_inc(s_vws[b % 2], 16)
            e.wait_ge(DV.sem, DV.done(0, ("k1", 1)))
            e.dma_start(kr_dram.rearrange("b p k -> p b k"), kr[:]).then_inc(s_krs, 16)
            for b in range(B):
                store_vw(b)
            e.dma_start(w1[:], W1).then_inc(s_w1, 16)
            e.wait_ge(s_krs, 16)
            for s in s_vws:
                e.wait_ge(s, 16 * B // 2)

        def pool_plan():
            def nh(e, i, w):
                for t, v in ((none_, -1.0), (eps_l, LN_EPS), (eps_r, RMS_EPS)):
                    e.memset(t[:], v)
                return e.memset(nhalf[:], -0.5)
            yield "nh", nh

            def m0(e, i, w):
                w(DV, ("ag", NC - 1))
                return e.tensor_tensor(ms[:], mv[:, :, 0], mv[:, :, 0], ALU.mult)
            yield "ms0", m0

            def m1(e, i, w):
                w(PO, "ms0")
                return e.tensor_tensor(ms2[:], ms[:], mv[:, :, 1], ALU.add)
            yield "ms1", m1

            def m2(e, i, w):
                w(PO, "ms1")
                return e.tensor_tensor(ms[:], ms2[:], eps_r[:, 0:NC], ALU.add)
            yield "ms2", m2

            def m3(e, i, w):
                w(PO, "ms2")
                return e.tensor_tensor(rr[:], ms[:], nhalf[:, 0:NC], ALU.pow)
            yield "ms3", m3

        @blk.gpsimd
        def _(e):
            run_steps(e, PO, list(pool_plan()))

        def act_plan():
            def gate(e, i, w):
                e.wait_ge(L["small"], count["small"])
                e.activation(gate_x[:], gts[:, 0:1], ACT.Tanh)
                return e.activation(gate_f[:], gts[:, 1:2], ACT.Tanh)
            yield "gate", gate
            for t in range(NC):
                def cn(e, i, w, t=t):
                    w(PO, "ms3")
                    return e.activation(cx[:, t, :], cx[:, t, :], ACT.Copy, scale=rr[:, t:t + 1])
                yield ("cn", t), cn
            for _, c, h in cT:
                def mn(e, i, w, c=c, h=h):
                    w(PE, ("cT", c, h))
                    return e.activation(mnT[:, c, h * HT:(h + 1) * HT], ps[:, 2 * c + h, :], ACT.Copy)
                yield ("mn", c, h), mn
            for h in range(2):
                def v(e, i, w, h=h):
                    w(PE, ("v", h))
                    return e.activation(vT[:, h * HT:(h + 1) * HT], ps[:, 4 + h, :], ACT.Copy)
                yield ("vT", h), v
            for b in range(B):
                for pr in range(2):
                    def vwe(e, i, w, b=b, pr=pr):
                        w(PE, ("vw", b, pr))
                        if b >= 2 and pr == 0:
                            e.wait_ge(s_vws[b % 2], 16 * (b // 2))
                        if b == 0:
                            w(AC, "gate")
                        return e.activation(vwb[:, b % 2, 0, pr, :], ps[:, 4 + 2 * (b % 2) + pr, :], ACT.Copy, scale=gate_x[:])
                    yield ("vwe", b, pr), vwe

        @blk.scalar
        def _(e):
            run_steps(e, AC, list(act_plan()))

        def dve_plan():
            def sc1(e, i, w):
                e.wait_ge(L["small"], count["small"])
                return e.tensor_scalar(rs1[:], rs1[:], 1.0, None, ALU.add)
            yield "sc1", sc1
            for t in range(NC):
                def s_(e, i, w, t=t):
                    e.wait_ge(L["ctx"], count["ctx"])
                    return e.bn_stats(bst[:, t, :], cx[:, t, :])
                yield ("st", t), s_
            for t in range(NC):
                def a_(e, i, w, t=t):
                    w(DV, ("st", t))
                    return e.bn_aggr(mv[:, t, :], bst[:, t, :])
                yield ("ag", t), a_
            for c in range(C):
                def qs(e, i, w, c=c):
                    e.wait_ge(L["qw"], count["qw"])
                    w(DV, "sc1")
                    v = qraw[:, c].rearrange("p n h -> p (n h)")
                    return e.tensor_scalar(v, v, rs1[:, c:c + 1], None, ALU.mult)
                yield ("qs", c), qs
            qf = qraw[:].rearrange("p c n h -> p (c n h)")

            def qhi(e, i, w):
                w(DV, ("qs", C - 1))
                return e.tensor_copy(qh[:].rearrange("p c n -> p (c n)"), qf)
            yield "qhi", qhi

            def qlo(e, i, w):
                w(DV, "qhi")
                return e.tensor_tensor(ql[:].rearrange("p c n -> p (c n)"), qf,
                                       qh[:].rearrange("p c n -> p (c n)").bitcast(F32), ALU.subtract)
            yield "qlo", qlo
            for c in range(C):
                def kv(e, i, w, c=c):
                    e.wait_ge(L["kvw"], count["kvw"])
                    return e.tensor_scalar(kvs[:, c, 0:2 * DH], kvraw[:, c, :], rs1[:, c:c + 1], None, ALU.mult)
                yield ("kvs", c), kv
            HH = DH // 2
            for k in range(2):
                for c in range(C):
                    def ks(e, i, w, c=c, k=k):
                        return e.tensor_scalar(kvs[:, c, 2 * DH + k * HH:2 * DH + (k + 1) * HH],
                                               kvraw[:, c, (1 - k) * HH:(2 - k) * HH], rs1[:, c:c + 1], None, ALU.mult)
                    yield (f"ks{k + 1}", c), ks
            yield "mkf", lambda e, i, w: e.tensor_copy(mkf[:], mk[:])

            def mkb(e, i, w):
                w(DV, "mkf")
                return e.tensor_scalar(kr[:, :, 2 * S], mkf[:], -FILL, FILL, ALU.mult, ALU.add)
            yield "mkb", mkb
            nb = HT // S
            for h in range(2):
                def tab(t):
                    return t[:, 0:S].unsqueeze(1).broadcast_to([P, nb, S])
                def krv(k):
                    return kr[:, h * nb:(h + 1) * nb, k * S:(k + 1) * S]
                def psv(w_, h=h):
                    return ps[:, 2 * w_ + h, :].rearrange("p (b s) -> p b s", s=S)
                kv0 = kt[:, 0, :].rearrange("p (b s) -> p b s", s=S)
                kv1 = kt[:, 1, :].rearrange("p (b s) -> p b s", s=S)
                k0v, k1v = krv(0), krv(1)

                def f1(e, i, w, h=h, o=kv0, a=psv(0), t=tab(cos)):
                    w(PE, ("k", 1, h))
                    e.wait_ge(L["tab"], count["tab"])
                    if h:
                        w(DV, ("k1", h - 1))
                    return e.tensor_tensor(o, a, t, ALU.mult)
                yield ("kC", h), f1
                yield ("sS", h), lambda e, i, w, h=h, o=kv1, a=psv(1), t=tab(sin): e.tensor_tensor(o, a, t, ALU.mult)

                def f3(e, i, w, h=h, o=k0v, a=kv0, b=kv1):
                    w(DV, ("sS", h))
                    return e.tensor_tensor(o, a, b, ALU.subtract)
                yield ("k0", h), f3

                def f4(e, i, w, h=h, o=kv0, a=psv(1), t=tab(cos)):
                    w(DV, ("k0", h))
                    return e.tensor_tensor(o, a, t, ALU.mult)
                yield ("sC", h), f4
                yield ("kS", h), lambda e, i, w, h=h, o=kv1, a=psv(0), t=tab(sin): e.tensor_tensor(o, a, t, ALU.mult)

                def f6(e, i, w, h=h, o=k1v, a=kv0, b=kv1):
                    w(DV, ("kS", h))
                    return e.tensor_tensor(o, a, b, ALU.add)
                yield ("k1", h), f6
            for b in range(B):
                for pr in range(2):
                    def vwl(e, i, w, b=b, pr=pr):
                        w(AC, ("vwe", b, pr))
                        return e.scalar_tensor_tensor(out=vwb[:, b % 2, 1, pr, :], in0=ps[:, 4 + 2 * (b % 2) + pr, :], scalar=gate_x[:],
                                                      in1=vwb[:, b % 2, 0, pr, :].bitcast(F32), op0=ALU.mult, op1=ALU.subtract)
                    yield ("vwl", b, pr), vwl

        @blk.vector
        def _(e):
            run_steps(e, DV, list(dve_plan()))

        def pe_plan():
            for _, c, h in cT:
                def f(e, i, w, c=c, h=h):
                    e.wait_ge(L["small"], count["small"])
                    w(AC, ("cn", 4 * h + 3))
                    for t in range(4):
                        last = e.transpose(ps[:, 2 * c + h, t * P:(t + 1) * P], cx[:, 4 * h + t, c * P:(c + 1) * P], ident[:])
                    return last
                yield ("cT", c, h), f
            for _, k, h in kj:
                def f(e, i, w, k=k, h=h):
                    w(AC, ("mn", C - 1, 1)); w(DV, ("ks2", C - 1))
                    for c in range(C):
                        last = e.matmul(ps[:, 2 * k + h, :], kvs[:, c, 2 * DH * k:2 * DH * k + DH],
                                        mnT[:, c, h * HT:(h + 1) * HT], start=(c == 0), stop=(c == C - 1))
                    return last
                yield ("k", k, h), f
            for _, h in vj:
                def f(e, i, w, h=h):
                    for c in range(C):
                        last = e.matmul(ps[:, 4 + h, :], kvs[:, c, DH:2 * DH],
                                        mnT[:, c, h * HT:(h + 1) * HT], start=(c == 0), stop=(c == C - 1))
                    return last
                yield ("v", h), f
            for _, b, pr in vwj:
                def f(e, i, w, b=b, pr=pr):
                    e.wait_ge(L["ow"], count["ow"])
                    w(DV, ("vwl", b - 2, pr)) if b >= 2 else w(AC, ("vT", 1))
                    for n in range(2):
                        last = e.matmul(ps[n * S:(n + 1) * S, 4 + 2 * (b % 2) + pr, :], vT[:, b * S:(b + 1) * S], ow[:, 2 * pr + n, :],
                                        start=True, stop=True)
                    return last
                yield ("vw", b, pr), f

        @blk.tensor
        def _(e):
            run_steps(e, PE, list(pe_plan()))


UNITS = 4


def attention(nc, sem, ps, ident, small, cos, sin, qh, ql, x, kr_dram, vw_dram, x1_dram):
    nhalf, none_, eps_l, eps_r = small
    st = ExitStack()
    with st:
        sb = lambda n, s, dt=F32: st.enter_context(nc.sbuf_tensor(n, s, dt))
        xin = sb("xin", [P, UNITS, TH, D])
        xh = sb("xh", [P, TH, D])
        xTh = sb("xTh", [P, C, HT], F32R)
        xTl = sb("xTl", [P, C, HT], F32R)
        qc = sb("qc", [P, H, HT])
        qs = sb("qs", [P, H, HT])
        lt = sb("lt", [P, 2, HT])
        lg = sb("lg", [P, 2, 512])
        pr_ = sb("pr", [P, 2, 512])
        pTh = sb("pTh", [P, 2, 512], F32R)
        pTl = sb("pTl", [P, 2, 512], F32R)
        kb = sb("kb", [P, 2, 2 * S + 1])
        vw = sb("vw", [P, 2, 2, 2, D], F32R)
        bst = sb("a_bst", [P, UNITS, TH, 6])
        mv = sb("a_mv", [P, UNITS, TH, 2])
        va, r1, vb, vc, r2, sc, nb = (sb(n, [P, UNITS, TH]) for n in ("va", "r1", "vb", "vc", "r2", "sc", "nb"))
        mx = sb("mx", [P, 2, 8])
        sm = sb("sm", [P, 2, 8])
        rc = sb("rc", [P, 2, 8])
        junk = sb("a_junk", [P, 1])

        stat_steps = ("st", "ag", "va", "r1", "vb", "vc", "vd", "r2", "sc", "ns", "nb")
        norm_steps = ("xh", "T", "hi", "lo")
        query_steps = ("Q", "qc", "qs", "L", "lt")

        def lead(n):
            u = n[1]
            return (n[0] == "x" or n[0] in stat_steps and u < 3 or n[0] in norm_steps and u < 2
                    or n[0] in query_steps and u < 1 or n[0] in ("kb", "vw") and u == 0)

        def at(wait):
            def f(who, what, *_):
                u = what[1]
                wait(who, (what[0], u % UNITS) + what[2:], -(u // UNITS))
            return f

        def pair(i):
            return slice(i, i + 1) if isinstance(i, int) else bass.ds(i, 1)

        def tokens(d, u):
            return d.rearrange("k (n p) d -> k p n d", p=P)[u // 2][:, (u % 2) * TH:(u % 2 + 1) * TH, :]

        def scratch(d, i, k):
            return d.rearrange("(r k) p n -> r k p n", k=2)[pair(i), k].rearrange("o p n -> (o p) n")

        pe, act, dve, pool, sync = {}, {}, {}, {}, {}
        for u in range(UNITS):
            def f(e, i, w, u=u):
                w(f"o{u}", ("xo", u), 1)
                return e.dma_start(xin[:, u], tokens(x.rearrange("(r k) t d -> r k t d", k=2)[pair(i)].rearrange("o k t d -> (o k) t d"), u))
            sync["x", u] = f

            def f(e, i, w, u=u):
                w("dve", ("rs", u, TH - 1))
                return e.dma_start(tokens(x1_dram[2 * i:2 * i + 2] if isinstance(i, int) else x1_dram[bass.ds(2 * i, 2)], u), xin[:, u])
            sync["xo", u] = f

            for t in range(TH):
                def f(e, i, w, u=u, t=t):
                    w(f"x{u}", ("x", u))
                    return e.bn_stats(bst[:, u, t, :], xin[:, u, t, :])
                dve["st", u, t] = f

                def f(e, i, w, u=u, t=t):
                    if t == 0:
                        w("pool", ("nb", u), 1)
                        w("dve", ("st", u, TH - 1))
                        e.memset(junk[:], 0.0)
                    return e.bn_aggr(mv[:, u, t, :], bst[:, u, t, :])
                dve["ag", u, t] = f

            var, mean = mv[:, u, :, 1], mv[:, u, :, 0]
            chain = [
                ("va", va[:, u], var, eps_l[:, 0:TH], ALU.add),
                ("r1", r1[:, u], va[:, u], nhalf[:, 0:TH], ALU.pow),
                ("vb", vb[:, u], var, r1[:, u], ALU.mult),
                ("vc", vc[:, u], vb[:, u], r1[:, u], ALU.mult),
                ("vd", vb[:, u], vc[:, u], eps_r[:, 0:TH], ALU.add),
                ("r2", r2[:, u], vb[:, u], nhalf[:, 0:TH], ALU.pow),
                ("sc", sc[:, u], r1[:, u], r2[:, u], ALU.mult),
                ("ns", vc[:, u], sc[:, u], none_[:, 0:TH], ALU.mult),
                ("nb", nb[:, u], mean, vc[:, u], ALU.mult),
            ]
            for k, (o, *ops) in enumerate(chain):
                def f(e, i, w, u=u, k=k, ops=ops, chain=chain):
                    if k:
                        w("pool", (chain[k - 1][0], u))
                    else:
                        w("dve", ("ag", u, TH - 1))
                        w("act", ("xh", u, TH - 1), 1)
                    return e.tensor_tensor(*ops)
                pool[o, u] = f
            norm_chain = [o for o, *_ in chain]

            for t in range(TH):
                def f(e, i, w, u=u, t=t):
                    w("pool", ("nb", u))
                    at(w)("pe", ("T", u - 1, C - 1))
                    return e.activation(xh[:, t, :], xin[:, u, t, :], ACT.Identity,
                                        scale=sc[:, u, t:t + 1], bias=nb[:, u, t:t + 1])
                act["xh", u, t] = f
            for c in range(C):
                def f(e, i, w, u=u, c=c):
                    w("act", ("xh", u, TH - 1))
                    at(w)("dve", ("lo", u, c - 2) if c >= 2 else ("rs", u - 3, 2 + c))
                    for t in range(TH):
                        last = e.transpose(ps[:, c % 2, t * P:(t + 1) * P], xh[:, t, c * P:(c + 1) * P], ident[:])
                    return last
                pe["T", u, c] = f

                def f(e, i, w, u=u, c=c):
                    w("pe", ("T", u, c))
                    return e.activation(xTh[:, c, :], ps[:, c % 2, :], ACT.Copy)
                act["hi", u, c] = f

                def f(e, i, w, u=u, c=c):
                    w("act", ("hi", u, c))
                    return e.tensor_tensor(xTl[:, c, :], ps[:, c % 2, :], xTh[:, c, :].bitcast(F32), ALU.subtract)
                dve["lo", u, c] = f
            for n in range(H):
                def f(e, i, w, u=u, n=n):
                    if n >= 2:
                        w("dve", ("qs", u, n - 2))
                    else:
                        w("dve", ("lo", u, C - 1))
                        at(w)("dve", ("qs", u - 1, n + 2))
                    parts = [(a, b, c) for c in range(C) for a, b in ((qh, xTh), (qh, xTl), (ql, xTh))]
                    for k, (a, b, c) in enumerate(parts):
                        last = e.matmul(ps[:, 2 + n % 2, :], a[:, c, n * DH:(n + 1) * DH], b[:, c, :],
                                        start=(k == 0), stop=(k == len(parts) - 1))
                    return last
                pe["Q", u, n] = f
                for o, tab, dst in (("qc", cos, qc), ("qs", sin, qs)):
                    def f(e, i, w, u=u, n=n, tab=tab, dst=dst):
                        w("pe", ("Q", u, n))
                        h = u % 2
                        return e.tensor_tensor(dst[:, n, :], ps[:, 2 + n % 2, :],
                                               tab[:, S + h * HT:S + (h + 1) * HT], ALU.mult)
                    dve[o, u, n] = f
            for p in range(2):
                def f(e, i, w, u=u, p=p):
                    w("dve", ("qs", u, 2 * p + 1))
                    at(w)("act", ("lt", u if p else u - 1, 1 - p))
                    w(f"k{u // 2}", ("kb", u // 2))
                    for k in range(2):
                        for n in range(2):
                            last = e.matmul(ps[n * S:(n + 1) * S, 4, :], kb[:, u // 2, k * S:(k + 1) * S],
                                            (qc, qs)[k][:, 2 * p + n, :], start=(k == 0), stop=(k == 1))
                    return last
                pe["L", u, p] = f

                def f(e, i, w, u=u, p=p):
                    w("pe", ("L", u, p))
                    return e.activation(lt[:, p, :], ps[:, 4, :], ACT.Identity,
                                        scale=float(DH) ** -0.5, bias=kb[:, u // 2, 2 * S:2 * S + 1])
                act["lt", u, p] = f

            def heads(v):
                return v.rearrange("p (a s) -> p a s", s=S)
            for tp in range(2):
                def f(e, i, w, u=u, tp=tp):
                    w("act", ("lt", u, 1))
                    at(w)("dve", ("sb", u - 1, tp))
                    for t in range(2):
                        for p in range(2):
                            last = e.transpose(ps[:, 5 + tp, (2 * t + p) * P:(2 * t + p + 1) * P],
                                               lt[:, p, (2 * tp + t) * P:(2 * tp + t + 1) * P], ident[:])
                    return last
                pe["LT", u, tp] = f

                def f(e, i, w, u=u, tp=tp):
                    w("pe", ("LT", u, tp))
                    return e.tensor_reduce(out=mx[:, tp, :], in_=heads(ps[:, 5 + tp, :]), op=ALU.max, axis=AX_X)
                dve["mx", u, tp] = f

                def f(e, i, w, u=u, tp=tp):
                    w("dve", ("mx", u, tp))
                    at(w)("pool", ("pr", u - 1, tp))
                    return e.tensor_tensor(heads(lg[:, tp, :]), heads(ps[:, 5 + tp, :]),
                                           mx[:, tp, :].unsqueeze(2).broadcast_to([P, 8, S]), ALU.subtract)
                dve["sb", u, tp] = f

                def f(e, i, w, u=u, tp=tp):
                    w("dve", ("sb", u, tp))
                    return e.activation(lg[:, tp, :], lg[:, tp, :], ACT.Exp)
                act["ex", u, tp] = f

                def f(e, i, w, u=u, tp=tp):
                    w("act", ("ex", u, tp))
                    return e.tensor_reduce(out=sm[:, tp, :], in_=heads(lg[:, tp, :]), op=ALU.add, axis=AX_X)
                dve["sm", u, tp] = f

                def f(e, i, w, u=u, tp=tp):
                    w("dve", ("sm", u, tp))
                    return e.reciprocal(rc[:, tp, :], sm[:, tp, :])
                dve["rc", u, tp] = f

                def f(e, i, w, u=u, tp=tp):
                    w("dve", ("rc", u, tp))
                    at(w)("pe", ("PT", u - 1, tp))
                    return e.tensor_tensor(heads(pr_[:, tp, :]), heads(lg[:, tp, :]),
                                           rc[:, tp, :].unsqueeze(2).broadcast_to([P, 8, S]), ALU.mult)
                pool["pr", u, tp] = f

                def f(e, i, w, u=u, tp=tp):
                    w("pool", ("pr", u, tp))
                    at(w)("dve", ("pl", u if tp else u - 1, 1 - tp))
                    for k in range(4):
                        last = e.transpose(ps[:, 7, k * P:(k + 1) * P], pr_[:, tp, k * P:(k + 1) * P], ident[:])
                    return last
                pe["PT", u, tp] = f

                def f(e, i, w, u=u, tp=tp):
                    w("pe", ("PT", u, tp))
                    return e.activation(pTh[:, tp, :], ps[:, 7, :], ACT.Copy)
                act["pT", u, tp] = f

                def f(e, i, w, u=u, tp=tp):
                    w("act", ("pT", u, tp))
                    return e.tensor_tensor(pTl[:, tp, :], ps[:, 7, :], pTh[:, tp, :].bitcast(F32), ALU.subtract)
                dve["pl", u, tp] = f
            for t in range(TH):
                def f(e, i, w, u=u, t=t):
                    w("dve", ("pl", u, t // 2)) if t < 2 else None
                    at(w)("dve", ("rs", u, t - 2) if t >= 2 else ("lo", u + 2, 2 + t))
                    w(f"v{u // 2}", ("vw", u // 2))
                    parts = [(a, k, p) for p in range(2) for a, k in ((pTh, 0), (pTh, 1), (pTl, 0))]
                    for m, (a, k, p) in enumerate(parts):
                        at_ = (2 * (t % 2) + p) * P
                        last = e.matmul(ps[:, t % 2, :], a[:, t // 2, at_:at_ + P], vw[:, u // 2, k, p, :],
                                        start=(m == 0), stop=(m == len(parts) - 1))
                    return last
                pe["PV", u, t] = f

                def f(e, i, w, u=u, t=t):
                    w("pe", ("PV", u, t))
                    return e.tensor_tensor(xin[:, u, t, :], ps[:, t % 2, :], xin[:, u, t, :], ALU.add)
                dve["rs", u, t] = f
        for k in range(2):
            def f(e, i, w, k=k):
                w("act", ("lt", 2 * k + 1, 1), 1)
                return e.dma_start(kb[:, k], scratch(kr_dram, i, k))
            sync["kb", k] = f

            def f(e, i, w, k=k):
                w("pe", ("PV", 2 * k + 1, TH - 1), 1)
                return e.dma_start(vw[:, k].rearrange("p r a d -> p (r a d)").bitcast(F32), scratch(vw_dram.rearrange("b p r a d -> b p (r a d)"), i, k))
            sync["vw", k] = f

        def order(parts):
            out = []
            for u in range(UNITS):
                for p in parts:
                    out.append((p[0], (u + p[1]) % UNITS) + tuple(p[2:]))
            return out

        pe_order = order([("LT", 0, 0), ("LT", 0, 1)] + [("Q", 1, n) for n in range(H)]
                         + [("T", 2, 0), ("T", 2, 1), ("L", 1, 0), ("T", 2, 2), ("T", 2, 3), ("PT", 0, 0), ("L", 1, 1), ("PT", 0, 1)]
                         + [("PV", 0, t) for t in range(TH)])
        act_order = order([("ex", 0, 0), ("ex", 0, 1)] + [("xh", 2, t) for t in range(TH)] + [("hi", 2, 0), ("hi", 2, 1)]
                          + [("lt", 1, 0), ("hi", 2, 2), ("hi", 2, 3), ("pT", 0, 0), ("lt", 1, 1), ("pT", 0, 1)])
        dve_order = order([("mx", 0, 0), ("sb", 0, 0), ("mx", 0, 1), ("sb", 0, 1), ("qc", 1, 0), ("qs", 1, 0),
                           ("sm", 0, 0), ("rc", 0, 0), ("sm", 0, 1), ("rc", 0, 1), ("qc", 1, 1), ("qs", 1, 1),
                           ("qc", 1, 2), ("qs", 1, 2), ("st", 3, 0), ("st", 3, 1), ("qc", 1, 3), ("qs", 1, 3)]
                          + [("lo", 2, c) for c in range(C)]
                          + [("pl", 0, 0), ("st", 3, 2), ("pl", 0, 1), ("rs", 0, 0), ("st", 3, 3), ("rs", 0, 1)]
                          + [("ag", 3, t) for t in range(TH)] + [("rs", 0, 2), ("rs", 0, 3)])
        pool_order = order([("pr", 0, 0), ("pr", 0, 1)] + [(o, 3) for o in norm_chain])
        sync_order = []
        for u in range(UNITS):
            sync_order += {0: [("kb", 1), ("vw", 1)], 2: [("kb", 0), ("vw", 0)]}.get(u, [])
            sync_order += [("xo", u), ("x", u)]
        plans = {"pe": (pe, pe_order), "act": (act, act_order), "dve": (dve, dve_order), "pool": (pool, pool_order),
                 "sync": (sync, sync_order)}
        slots = {f"x{u}": [("x", u)] for u in range(UNITS)}
        slots |= {f"k{k}": [("kb", k)] for k in range(2)} | {f"v{k}": [("vw", k)] for k in range(2)}
        slots |= {f"o{u}": [("xo", u)] for u in range(UNITS)}
        Phase(nc, sem, "a", {k: [(n, d[n]) for n in o] for k, (d, o) in plans.items()}, slots, lead, B // 2)


def experts(nc, sem, ps, w1, ident, small, gate_f, s_w1, Wc, bc, b1, b2, tie_in, gmask_in,
            x1_dram, w2_dram, out):
    nhalf, none_, eps_l, eps_r = small
    st = ExitStack()
    with st:
        sb = lambda n, s, dt=F32: st.enter_context(nc.sbuf_tensor(n, s, dt))
        QH = Q // 2
        GB = NT // 2
        NB = Q // QB
        wc = sb("wc", [P, C, E])
        bcol = sb("bcol", [P, 1])
        b1c = sb("b1c", [P, Q])
        b2s = sb("b2s", [P, D])
        tie = sb("tie", [P, G])
        gmask = sb("gmask", [P, GT])
        identb = sb("identb", [P, P], BF16)
        w2s = sb("w2s", [P, 4, QB * P])
        xin = sb("b_xin", [P, 4, D])
        xf = sb("xf", [P, 2, D])
        xnh = sb("xnh", [P, NT, D], F32R)
        xnl = sb("xnl", [P, NT, D], F32R)
        gat = sb("gat", [P, 2, QH * 4 * NG])
        xT = gat[:].rearrange("p h (c t) -> p h c t", t=HT)
        lgt = sb("lgt", [P, HT])
        hb = lgt
        top_ = sb("top", [P, HT // G])
        selT = sb("selT", [P, T])
        selN = sb("selN", [P, T], BF16)
        sel = sb("sel", [P, NT, P], BF16)
        selb = sb("selb", [P, NT, QH * 4 * GT], F32R)
        hid = sb("hid", [P, Q, 4 * NG])
        res = sb("res", [P, 2, Q * P])
        y = sb("y", [P, 2, 4, P])
        bst = sb("b_bst", [P, NT, 6])
        mv = sb("b_mv", [P, NT, 2])
        va, r1, ns, nb = (sb(n, [P, NT // 2, 2]) for n in ("b_va", "b_r1", "b_ns", "b_nb"))
        junk = sb("b_junk", [P, 1])

        consts = [(wc, Wc.rearrange("(c p) e s -> p c (e s)", p=P)), (bcol, bc), (b1c, b1),
                  (b2s, b2.rearrange("e s d -> (e s) d")), (tie, tie_in.partition_broadcast(P)), (gmask, gmask_in)]
        s_c = sem("b_const")
        s_m = sem("b_set")
        with nc.Block() as blk:
            @blk.sync
            def _(e):
                for o, v in consts:
                    e.dma_start(o[:], v).then_inc(s_c, 16)
                e.wait_ge(s_c, 16 * len(consts))
                e.wait_ge(s_w1, 16)

            @blk.vector
            def _(e):
                e.memset(hid[:], 0.0)
                e.tensor_copy(identb[:], ident[:]).then_inc(s_m, 1)

        rooms = {"res0": res[:, 1, 0:4 * QB * P], "res1": res[:, 1, 4 * QB * P:8 * QB * P],
                 "half0": gat[:, 0, :], "half1": gat[:, 1, :]}
        kinds = ["own", "res0", "res1", "own", "half0", "own", "half1", "own"]

        def piece(n):
            kind, k = kinds[n // 4], n % 4
            if kind == "own":
                return ("w2", n), w2s[:, k, :]
            return ("w2", n - k), rooms[kind][:, k * QB * P:(k + 1) * QB * P]

        def slot(n):
            return f"w_{kinds[n // 4]}" + (str(n % 4) if kinds[n // 4] == "own" else "")

        loads = sorted({piece(n)[0][1] for n in range(NB * C)})

        LEAD = {"x", "st", "ag", "va", "r1", "ns", "nb", "lo", "xf", "hi", "T", "xT", "lg", "mx", "eq", "sT", "sel"}

        def lead(n):
            return n[0] in LEAD or n[0] == "sp" and n[1] == 0 or n[:3] == ("ga", 0, 0)

        def batch(d, i, t0, n):
            d = d[i:i + 1] if isinstance(i, int) else d[bass.ds(i, 1)]
            return d.rearrange("o (n p) d -> p (o n) d", p=P)[:, t0:t0 + n, :]

        front = ([("T", t) for t in range(4)] + [("lg", 0)] + [("T", t) for t in range(4, 8)]
                 + [("lg", 1), ("sT", 0), ("sT", 1)])
        reader = {"T": ("act", "xT"), "lg": ("dve", "lg"), "sT": ("act", "sel")}
        front_bank = {n: 2 + k % 2 for k, n in enumerate(front)}

        def bank_read(w, n):
            k = front.index(n)
            if k >= 2:
                eng, o = reader[front[k - 2][0]]
                return w(eng, (o, front[k - 2][1]))
            return w("dve", ("hr", 1, 2 + k), 1)

        def sbank(c, h):
            return h + 2 * (c == C - 1)

        def normed(t):
            return "xf" if t in (2, 3) else "hi"

        pe, act, dve, pool, sync = {}, {}, {}, {}, {}
        for t in range(NT):
            def f(e, i, w, t=t):
                w("act", (normed(t - 4), (t - 4) % NT), int(t < 4))
                return e.dma_start(xin[:, t % 4, :], batch(x1_dram, i, t, 1)[:, 0])
            sync["x", t] = f

            def f(e, i, w, t=t):
                w(f"x{t % 4}", ("x", t))
                return e.bn_stats(bst[:, t, :], xin[:, t % 4, :])
            dve["st", t] = f

            def f(e, i, w, t=t):
                if t % 2 == 0:
                    w("pool", ("nb", t // 2), 1)
                    w("dve", ("st", t + 1))
                    e.memset(junk[:], 0.0)
                return e.bn_aggr(mv[:, t, :], bst[:, t, :])
            dve["ag", t] = f

            def f(e, i, w, t=t, k=t // 2, j=t % 2):
                w("pool", ("lo", t - 2) if t >= 2 else ("nb", k))
                w("pool", ("nb", k))
                w("pe", ("T", (t - 2) % NT), int(t < 2))
                if t < 2:
                    w("pool", ("lo", t - 2 + NT), 1)
                return e.activation(xf[:, j, :], xin[:, t % 4, :], ACT.Identity, scale=r1[:, k, j:j + 1], bias=nb[:, k, j:j + 1])
            act["xf", t] = f

            def f(e, i, w, t=t, k=t // 2, j=t % 2):
                w("pe", ("ga", 1, C - 1, GB - 1), 1)
                w("pool", ("nb", k))
                return e.activation(xnh[:, t, :], xin[:, t % 4, :], ACT.Identity, scale=r1[:, k, j:j + 1], bias=nb[:, k, j:j + 1])
            act["hi", t] = f

            def f(e, i, w, t=t):
                w("act", (normed(t), t))
                return e.tensor_tensor(xnl[:, t, :], xf[:, t % 2, :], xnh[:, t, :].bitcast(F32), ALU.subtract)
            pool["lo", t] = f

            def f(e, i, w, t=t):
                n = ("T", t)
                if t == TH:
                    bank_read(w, n)
                w("act", ("xf", t))
                bank_read(w, n)
                for c in range(C):
                    last = e.transpose(ps[:, front_bank[n], c * P:(c + 1) * P], xf[:, t % 2, c * P:(c + 1) * P], ident[:])
                return last
            pe["T", t] = f

            def f(e, i, w, t=t):
                w("pe", ("T", t))
                return e.activation(xT[:, t // TH, :, (t % TH) * P:(t % TH + 1) * P],
                                    ps[:, front_bank["T", t], :].rearrange("p (c t) -> p c t", t=P), ACT.Copy)
            act["xT", t] = f
        for k in range(NT // 2):
            var, mean = mv[:, 2 * k:2 * k + 2, 1], mv[:, 2 * k:2 * k + 2, 0]
            chain = [("va", va[:, k], var, eps_l[:, 0:2], ALU.add), ("r1", r1[:, k], va[:, k], nhalf[:, 0:2], ALU.pow),
                     ("ns", ns[:, k], r1[:, k], none_[:, 0:2], ALU.mult), ("nb", nb[:, k], mean, ns[:, k], ALU.mult)]
            for m, (o, *ops) in enumerate(chain):
                def f(e, i, w, k=k, m=m, ops=ops, chain=chain):
                    if m:
                        w("pool", (chain[m - 1][0], k))
                    else:
                        w("dve", ("ag", 2 * k + 1))
                        w("act", (normed(2 * k + 1), 2 * k + 1), 1)
                    return e.tensor_tensor(*ops)
                pool[o, k] = f
        for h in range(2):
            def groups(v):
                return v.rearrange("p (n t) -> p n t", t=G)

            def f(e, i, w, h=h):
                w("act", ("xT", h * TH + TH - 1))
                bank_read(w, ("lg", h))
                for c in range(C):
                    last = e.matmul(ps[:, front_bank["lg", h], :], wc[:, c, :], xT[:, h, c, :], start=(c == 0), stop=(c == C - 1))
                return last
            pe["lg", h] = f

            def f(e, i, w, h=h):
                w("pe", ("lg", h))
                w("dve", ("eq", 0) if h else ("hr", 1, 3), 0 if h else 1)
                return e.scalar_tensor_tensor(out=groups(lgt[:]), in0=groups(ps[:, front_bank["lg", h], :]), scalar=bcol[:],
                                              in1=tie[:].unsqueeze(1).broadcast_to([P, HT // G, G]), op0=ALU.add, op1=ALU.add)
            dve["lg", h] = f

            def f(e, i, w, h=h):
                w("dve", ("lg", h))
                return e.tensor_reduce(out=top_[:], in_=groups(lgt[:]), op=ALU.max, axis=AX_X)
            dve["mx", h] = f

            def f(e, i, w, h=h):
                w("dve", ("mx", h))
                w("act", ("cp", h), 1)
                return e.tensor_tensor(groups(selN[:, h * HT:(h + 1) * HT]), groups(lgt[:]),
                                       top_[:].unsqueeze(2).broadcast_to([P, HT // G, G]), ALU.is_equal)
            dve["eq", h] = f

            def f(e, i, w, h=h):
                w("pe", ("sc", C - 1, 1), 1)
                w("dve", ("eq", h))
                return e.activation(selT[:, h * HT:(h + 1) * HT], selN[:, h * HT:(h + 1) * HT], ACT.Copy)
            act["cp", h] = f

            def f(e, i, w, h=h):
                w("dve", ("eq", h))
                bank_read(w, ("sT", h))
                b = ps[:, front_bank["sT", h], :].bitcast(BF16)
                for t in range(TH):
                    last = e.transpose(b[:, t * P:(t + 1) * P], selN[:, (h * TH + t) * P:(h * TH + t + 1) * P], identb[:])
                return last
            pe["sT", h] = f

            def f(e, i, w, h=h):
                w("pe", ("sT", h))
                w("pool", ("sp", 1, NT - 1), 1)
                b = ps[:, front_bank["sT", h], :].bitcast(BF16)[:, 0:HT]
                return e.activation(sel[:, h * TH:(h + 1) * TH, :].rearrange("p t e -> p (t e)"), b, ACT.Copy)
            act["sel", h] = f
        for eh in range(2):
            for t in range(NT):
                def f(e, i, w, eh=eh, t=t):
                    w("act", ("sel", t // TH))
                    w("pe", ("ga", 1 - eh, C - 1, t // 2), 1 - eh)
                    v = sel[:, t, :].rearrange("p (j q) -> p q j", q=Q)[:, eh * QH:(eh + 1) * QH, :]
                    return e.tensor_tensor(selb[:, t, :].rearrange("p (q j g) -> p q j g", j=4, g=GT),
                                           v.unsqueeze(3).broadcast_to([P, QH, 4, GT]),
                                           gmask[:].unsqueeze(1).unsqueeze(1).broadcast_to([P, QH, 4, GT]), ALU.mult)
                pool["sp", eh, t] = f
            for c in range(C):
                for k in range(GB):
                    who = "dve" if k % 2 else "act"

                    def f(e, i, w, eh=eh, c=c, k=k, who=who):
                        w("pool", ("sp", eh, 2 * k + 1))
                        if eh == 0 and c == 0:
                            w("pool", ("lo", NT - 1))
                            w("act", ("rs", C - 1, 4 + k), 1)
                        else:
                            w(who, ("ga", eh, c - 1, k) if c else ("ga", 0, C - 1, k))
                        for t in range(2):
                            for m, part in enumerate((xnh, xnl)):
                                last = e.matmul(ps[:, 4 + k, t * 256:(t + 1) * 256], part[:, 2 * k + t, c * P:(c + 1) * P],
                                                selb[:, 2 * k + t, :], start=(m == 0), stop=(m == 1))
                        return last
                    pe["ga", eh, c, k] = f

                    def f(e, i, w, eh=eh, c=c, k=k, who=who):
                        w("pe", ("ga", eh, c, k))
                        if c >= 2 or eh:
                            w("pe", ("w1", eh, c - 2, 3) if c >= 2 else ("w1", 0, c + 2, 3))
                        dst = gat[:, c % 2, :].rearrange("p (qj t g) -> p t qj g", t=NT, g=GT)[:, 2 * k:2 * k + 2]
                        src = ps[:, 4 + k, :].rearrange("p (t qj g) -> p t qj g", t=2, g=GT)
                        return e.tensor_copy(dst, src) if who == "dve" else e.activation(dst, src, ACT.Copy)
                    (dve if k % 2 else act)["ga", eh, c, k] = f

                for b in range(4):
                    def f(e, i, w, eh=eh, c=c, b=b):
                        if c == 0 and eh:
                            w("dve", ("hb", 0, b))
                        elif c == 0:
                            w("dve", ("fin", C - 1, 1), 1)
                        else:
                            w("dve", ("ga", eh, c, GB - 1))
                        w("act", ("ga", eh, c, GB - 2))
                        for q in range(QB * b, QB * (b + 1)):
                            last = e.matmul(ps[:, b, (q % QB) * P:(q % QB + 1) * P],
                                            w1[:, c, (eh * QH + q) * P:(eh * QH + q + 1) * P], gat[:, c % 2, q * P:(q + 1) * P],
                                            start=(c == 0 and q % QB == 0), stop=(c == C - 1), skip_group_check=True)
                        return last
                    pe["w1", eh, c, b] = f
            for b in range(4):
                q0 = eh * QH + b * QB

                def f(e, i, w, eh=eh, b=b, q0=q0):
                    w("pe", ("w1", eh, C - 1, b))
                    w("dve", ("hr", eh, b - 1) if b else ("hr", 0, 3) if eh else ("eq", 1))
                    return e.tensor_tensor(hb[:].rearrange("p (q n) -> p q n", n=P), ps[:, b, :].rearrange("p (q n) -> p q n", n=P),
                                           b1c[:, q0:q0 + QB].unsqueeze(2).broadcast_to([P, QB, P]), ALU.add)
                dve["hb", eh, b] = f

                def f(e, i, w, eh=eh, b=b, q0=q0):
                    w("dve", ("hb", eh, b))
                    if eh == 0 and b == 0:
                        w("pe", ("w2", C - 1, NB - 1), 1)
                    for j in range(4):
                        last = e.tensor_scalar(hid[j * F:(j + 1) * F, q0:q0 + QB, j * NG:(j + 1) * NG],
                                               hb[j * F:(j + 1) * F, :].rearrange("p (q n) -> p q n", n=P)[:, :, j * NG:(j + 1) * NG],
                                               0.0, None, ALU.max)
                    return last
                dve["hr", eh, b] = f
        for n in loads:
            def f(e, i, w, n=n):
                kind = kinds[n // 4]
                if kind == "own":
                    own = [m for m in loads if kinds[m // 4] == "own" and m % 4 == n % 4]
                    m = own[own.index(n) - 1]
                    w("pe", ("w2", m // NB, m % NB), int(n < 4))
                    return e.dma_start(piece(n)[1], w2_dram[n // NB, n % NB])
                if kind[:3] == "res":
                    w("pe", ("sc", C - 1, 1), 1)
                else:
                    h = int(kind[-1])
                    w("pe", ("lg", h), -1)
                    w("pe", ("w1", 1, C - 2 + h, 3))
                return e.dma_start(rooms[kind].rearrange("p (b k) -> p b k", b=4),
                                   w2_dram[n // NB, n % NB:n % NB + 4].rearrange("b p k -> p b k"))
            sync["w2", n] = f
        for c in range(C):
            for b in range(NB):
                def f(e, i, w, c=c, b=b):
                    n = NB * c + b - 4
                    load, place = piece(NB * c + b)
                    w(slot(NB * c + b), load)
                    if n >= 0:
                        w("act", ("rs", n // NB, n % NB))
                    else:
                        w("dve" if b % 2 else "act", ("ga", 1, C - 1, b))
                    if c == 0 and (n >= 0 or b % 2 == 0):
                        w("dve", ("hr", b // 4, b % 4))
                    for j in range(QB):
                        q = QB * b + j
                        last = e.matmul(ps[:, 4 + b % 4, j * P:(j + 1) * P], hid[:, q, :],
                                        place[:, j * P:(j + 1) * P], start=True, stop=True)
                    return last
                pe["w2", c, b] = f

                def f(e, i, w, c=c, b=b):
                    w("pe", ("w2", c, b))
                    return e.activation(res[:, c % 2, b * 512:(b + 1) * 512], ps[:, 4 + b % 4, :], ACT.Copy)
                act["rs", c, b] = f

            def f(e, i, w, c=c):
                w("act", ("rs", c, NB - 1))
                v = res[:, c % 2, :].rearrange("p (q d) -> p d q", d=P)
                return e.transpose(v, v)
            dve["tr", c] = f
            for h in range(2):
                def f(e, i, w, c=c, h=h):
                    w("dve", ("fin", c - 1, h) if 0 < c < C - 1 else ("tr", c))
                    w("dve", ("tr", c))
                    if c == C - 1:
                        w("act", ("sel", 1), -1)
                    w("act", ("cp", h))
                    r = res[:, c % 2, :].rearrange("p (g d) -> p g d", d=P)
                    for t in range(TH):
                        tt = h * TH + t
                        e.matmul(ps[:, sbank(c, h), t * P:(t + 1) * P], selT[:, tt * P:(tt + 1) * P], b2s[:, c * P:(c + 1) * P],
                                 start=(t == 0), stop=False, skip_group_check=True)
                        for g in range(GT):
                            last = e.matmul(ps[g * G:(g + 1) * G, sbank(c, h), t * P:(t + 1) * P],
                                            selT[:, tt * P + g * G:tt * P + (g + 1) * G], r[:, tt * GT + g, :],
                                            start=False, stop=(t == TH - 1 and g == GT - 1), skip_group_check=True)
                    return last
                pe["sc", c, h] = f

                def f(e, i, w, c=c, h=h):
                    w("pe", ("sc", c, h))
                    w(f"y{h}", ("yl", c, h))
                    v = y[:, h].rearrange("p t d -> p (t d)")
                    return e.scalar_tensor_tensor(out=v, in0=ps[:, sbank(c, h), :], scalar=gate_f[:], in1=v, op0=ALU.mult, op1=ALU.add)
                dve["fin", c, h] = f

                def f(e, i, w, c=c, h=h):
                    w(f"s{h}", ("ys", (c - 1) % C, h), int(c == 0))
                    return e.dma_start(y[:, h], batch(x1_dram, i, h * TH, TH)[:, :, c * P:(c + 1) * P])
                sync["yl", c, h] = f

                def f(e, i, w, c=c, h=h):
                    w("dve", ("fin", c, h))
                    return e.dma_start(batch(out, i, h * TH, TH)[:, :, c * P:(c + 1) * P], y[:, h])
                sync["ys", c, h] = f

        ga = lambda eh, c, ks: [("ga", eh, c, k) for k in ks]
        allk, evenk, oddk = range(GB), range(0, GB, 2), range(1, GB, 2)

        pe_order, prev = [], None
        for eh in range(2):
            for c in range(C):
                if (eh, c) != (0, 0):
                    pe_order += ga(eh, c, allk)
                if prev:
                    pe_order += [("w1",) + prev + (b,) for b in range(4)]
                prev = (eh, c)
        pe_order += [("w1",) + prev + (b,) for b in range(4)]
        after = {(0, 1): [("T", 0)], (0, 3): [("T", 1)], (0, 5): [("T", 2)], (0, 7): [("T", 3)],
                 (1, 1): [("lg", 0)], (1, 2): [("T", 4)], (1, 4): [("T", 5)], (1, 6): [("T", 6)], (2, 0): [("T", 7)],
                 (2, 2): [("lg", 1)], (2, 7): [("sT", 0)], (3, 0): [("sT", 1)]}
        for c in range(C):
            for b in range(NB):
                pe_order.append(("w2", c, b))
                pe_order += after.get((c, b), [])
            if c:
                pe_order += [("sc", c - 1, h) for h in range(2)]
        pe_order += ga(0, 0, allk) + [("sc", C - 1, h) for h in range(2)]

        act_order = [("cp", 0), ("cp", 1)]
        for eh in range(2):
            for c in range(C):
                if (eh, c) != (0, 0):
                    act_order += ga(eh, c, evenk)
        act_order += [(o, t) for t in range(2) for o in ("xf", "hi")] + [("hi", 2), ("hi", 3)]
        copies = []
        for c in range(C):
            for b in range(NB):
                copies.append(("rs", c, b))
                for o, *k in after.get((c, b), []):
                    if o == "T":
                        t = k[0]
                        copies.append(("xT", t))
                        if t + 2 < NT:
                            copies += [("xf", t + 2)] + ([("hi", t + 2)] if t + 2 >= 4 else [])
                    if o == "sT":
                        copies.append(("sel", k[0]))
        act_order += copies + ga(0, 0, evenk)

        dve_order = []
        for eh in range(2):
            for c in range(C):
                if (eh, c) != (0, 0):
                    dve_order += ga(eh, c, oddk)
                if (eh, c) == (0, 2):
                    dve_order += [("st", 0), ("st", 1), ("ag", 0), ("ag", 1), ("st", 2), ("st", 3), ("ag", 2), ("ag", 3)]
                if (eh, c) == (1, 0):
                    dve_order += [(o, 0, b) for b in range(4) for o in ("hb", "hr")]
        dve_order += [(o, 1, b) for b in range(4) for o in ("hb", "hr")]
        dve_order += [("st", 4), ("st", 5), ("ag", 4), ("ag", 5), ("st", 6), ("st", 7), ("ag", 6), ("ag", 7)]
        dve_order += [("tr", 0), ("lg", 0), ("mx", 0), ("eq", 0), ("tr", 1), ("fin", 0, 0), ("fin", 0, 1),
                      ("lg", 1), ("mx", 1), ("eq", 1), ("tr", 2), ("fin", 1, 0), ("fin", 1, 1), ("tr", 3),
                      ("fin", 2, 0), ("fin", 2, 1)] + ga(0, 0, oddk) + [("fin", 3, 0), ("fin", 3, 1)]

        pool_order = [("sp", 1, t) for t in range(NT)]
        norm = lambda k: [(o, k) for o in ("va", "r1", "ns", "nb")]
        pool_order += norm(0) + norm(1) + [("lo", 0), ("lo", 1)] + norm(2) + [("lo", 2), ("lo", 3)] + norm(3)
        pool_order += [("lo", t) for t in range(4, 8)] + [("sp", 0, t) for t in range(NT)]

        w2 = lambda *ns: [("w2", n) for n in ns]
        sync_order = [("x", t) for t in range(4)] + w2(0, 1, 2, 3) + [("yl", 0, 0), ("yl", 0, 1)] + w2(4, 8)
        ys = lambda c: [("ys", c, h) for h in range(2)]
        yl = lambda c: [("yl", c, h) for h in range(2)]
        sync_order += [("x", 4), ("x", 5), ("x", 6)] + w2(12, 13, 14, 15) + [("x", 7)] + w2(16) + ys(0) + w2(20, 21, 22)
        sync_order += yl(1) + w2(23, 24, 28, 29, 30, 31) + ys(1) + yl(2) + ys(2) + yl(3) + ys(3)

        slots = {f"x{k}": [("x", k), ("x", k + 4)] for k in range(4)}
        for n in loads:
            slots.setdefault(slot(n), []).append(("w2", n))
        slots |= {f"y{h}": [("yl", c, h) for c in range(C)] for h in range(2)}
        slots |= {f"s{h}": [("ys", c, h) for c in range(C)] for h in range(2)}
        plans = {"pe": (pe, pe_order), "act": (act, act_order), "dve": (dve, dve_order), "pool": (pool, pool_order),
                 "sync": (sync, sync_order)}
        Phase(nc, sem, "b", {k: [(n, d[n]) for n in o] for k, (d, o) in plans.items()}, slots, lead, B)


def kernel(x, ctx_1024, mask_BxS2_bk0, g_xattn, g_ffn, L0_xattn_rms_scale, L0_xattn_q_w, L0_xattn_kv_w,
           L0_xattn_out_w, L0_ffn_Wc, L0_ffn_bc, L0_ffn_W1, L0_ffn_b1, L0_ffn_W2, L0_ffn_b2):
    from concourse import bacc
    from concourse.bass_utils import run_bass_kernel_spmd

    half = np.arange(DH // 2, dtype=np.float32)
    scale = np.float32(10000.0) ** (np.float32(2.0 / DH) * half)
    angle = np.arange(S + T, dtype=np.float32)[None, :] / scale[:, None]
    cos = np.concatenate([np.cos(angle), np.cos(angle)]).astype(np.float32)
    sin = np.concatenate([np.sin(angle), -np.sin(angle)]).astype(np.float32)
    tie = np.linspace(0.0, 1e-6, G, dtype=np.float32)
    gmask = np.repeat(np.eye(GT, dtype=np.float32), G, axis=0)

    w1 = np.asarray(L0_ffn_W1).reshape(4, Q, C, P, F).transpose(3, 2, 1, 0, 4).reshape(P, C, E * F)
    w2 = np.asarray(L0_ffn_W2).reshape(4, Q // QB, QB, C, P, F).transpose(3, 1, 0, 5, 2, 4).reshape(C, Q // QB, P, QB * P)
    b1 = np.asarray(L0_ffn_b1).reshape(4, Q, F).transpose(0, 2, 1).reshape(P, Q)

    arrays = {
        "x": x, "ctx_1024": ctx_1024, "mask": np.asarray(mask_BxS2_bk0).T, "g_xattn": g_xattn, "g_ffn": g_ffn,
        "rms": np.asarray(L0_xattn_rms_scale).reshape(C, P).T, "q_w": L0_xattn_q_w, "kv_w": L0_xattn_kv_w, "out_w": L0_xattn_out_w,
        "Wc": L0_ffn_Wc, "bc": np.asarray(L0_ffn_bc).reshape(E, 1), "W1": w1, "b1": b1, "W2": w2, "b2": L0_ffn_b2,
        "ident": np.eye(P, dtype=np.float32), "cos": cos, "sin": sin, "tie": tie, "gmask": gmask,
    }
    arrays = {n: np.ascontiguousarray(a) for n, a in arrays.items()}
    nc = bacc.Bacc("TRN2", target_bir_lowering=False, num_devices=1)
    args = [nc.dram_tensor(f"in_{n}", a.shape, mybir.dt.from_np(a.dtype), kind="ExternalInput").ap() for n, a in arrays.items()]
    out = nc.dram_tensor("out", (B, T, D), F32, kind="ExternalOutput").ap()
    build(nc, *args, out)
    r = run_bass_kernel_spmd(nc, [{f"in_{n}": a for n, a in arrays.items()}], core_ids=[0])
    return r.results[0]["out"]
```

```python
from contextlib import ExitStack

import numpy as np

import concourse.bass as bass
from concourse import mybir
from concourse.alu_op_type import AluOpType as ALU

F32 = mybir.dt.float32
F32R = mybir.dt.float32r
BF16 = mybir.dt.bfloat16
U8 = mybir.dt.uint8
ACT = mybir.ActivationFunctionType
AX_X = mybir.AxisListType.X

P = 128
B, T, D = 16, 1024, 512
S = 64
H, DH = 4, 128
E, G = 128, 32
F = 32
C = D // P
NT = T // P
TH = NT // 2
HT = T // 2
GT = P // G
NG = T // G
Q = E // 4
QB = 4
FILL = -2.3819763e38
LN_EPS, RMS_EPS = 1e-5, 1e-6


class Steps:

    def __init__(self, sem, names, unit=1):
        self.sem, self.per, self.unit = sem, len(names), unit
        self.place = {n: k + 1 for k, n in enumerate(names)}
        assert len(self.place) == self.per

    def done(self, i, name, back=0):
        return i * (self.unit * self.per) + self.unit * ((1 - back) * self.per + self.place[name])


def run_steps(eng, steps, plan):
    for name, fn in plan:
        seen = {}

        def wait(who, what, back=0):
            at = who.done(0, what, back)
            if id(who) in seen:
                assert at <= seen[id(who)], (name, what)
                return
            seen[id(who)] = at
            eng.wait_ge(who.sem, at)
        fn(eng, 0, wait).then_inc(steps.sem, 1)


class Phase:

    def __init__(self, nc, sem, label, plans, slots, lead, rounds, ready=()):
        self.nc, self.plans, self.slots, self.lead, self.rounds = nc, plans, slots, lead, rounds
        self.looped = {}
        self.slot_of = {n: k for k, names in slots.items() for n in names}
        for kind, keep, over in (("first", lambda n: lead(n) and n[0] not in ready, (-1,)), ("loop", lambda n: True, (0, rounds - 1)),
                                 ("last", lambda n: not lead(n), (rounds - 1,))):
            self.block(sem, label + kind, kind, keep, over)

    def block(self, sem, label, kind, keep, over):
        tracks = {}
        for k, plan in self.plans.items():
            if k != "sync":
                tracks[k] = Steps(sem(f"{label}_{k}"), [n for n, _ in plan if keep(n)])
        for k, names in self.slots.items():
            tracks[k] = Steps(sem(f"{label}_{k}"), [n for n in names if keep(n)], unit=16)

        if kind == "loop":
            self.looped = tracks

        def emit(eng, key, i):
            for name, fn in self.plans[key]:
                if not keep(name):
                    continue
                seen = {}
                ahead = int(self.lead(name))

                def wait(who, what, ago=0):
                    back = ago + int(self.lead(what)) - ahead
                    if kind == "last" and back == 1 and who in self.slots:
                        t = self.looped[who]
                        eng.wait_ge(t.sem, t.done(self.rounds - 2, what, 0))
                        return
                    if kind != "loop" and (back or what not in tracks[who].place):
                        assert back >= 0
                        return
                    if back >= 2:
                        raise AssertionError((name, what, "too old"))
                    assert back >= 0, (name, what, "is in the future")
                    at = tracks[who].done(0, what, back)
                    if who in seen:
                        assert at <= seen[who], (name, who, what)
                        return
                    seen[who] = at
                    base = i if kind == "loop" else -1
                    eng.wait_ge(tracks[who].sem, tracks[who].done(base, what, back))
                last = fn(eng, i + ahead, wait)
                t = tracks[self.slot_of[name] if key == "sync" else key]
                last.then_inc(t.sem, t.unit)

        def program(key, eng):
            if key == "sync":
                if kind == "loop":
                    for t in tracks.values():
                        eng.sem_inc(t.sem, t.unit * t.per)
            if kind == "loop":
                with eng.Fori(*over) as i:
                    emit(eng, key, i)
            else:
                emit(eng, key, over[0])
            if key == "sync" and kind != "loop":
                for k in self.slots:
                    if kind == "last":
                        t = self.looped[k]
                        eng.wait_ge(t.sem, t.unit * t.per * self.rounds)
                    if tracks[k].per:
                        eng.wait_ge(tracks[k].sem, tracks[k].unit * tracks[k].per)

        with self.nc.Block() as blk:
            blk.sync(lambda e: program("sync", e))
            blk.gpsimd(lambda e: program("pool", e))
            blk.scalar(lambda e: program("act", e))
            blk.vector(lambda e: program("dve", e))
            blk.tensor(lambda e: program("pe", e))


def build(nc, x, ctx_in, mask, gx_in, gf_in, rms, q_w, kv_w, out_w, Wc, bc, W1, b1, W2, b2,
          ident_in, cos_in, sin_in, tie_in, gmask_in, out):
    x1_dram = nc.dram_tensor("x1_scratch", (B, T, D), F32, kind="Internal").ap()
    kr_dram = nc.dram_tensor("k_scratch", (B, P, 2 * S + 1), F32, kind="Internal").ap()
    vw_dram = nc.dram_tensor("vw_scratch", (B, P, 2, D), F32, kind="Internal").ap()

    top = ExitStack()

    def sem(name):
        return top.enter_context(nc.semaphore(name))

    with top:
        ps = top.enter_context(nc.psum_tensor("ps", [P, 8, 512], F32))
        sb0 = lambda n, s, dt=F32: top.enter_context(nc.sbuf_tensor(n, s, dt))
        w1 = sb0("w1", [P, C, E * F])
        ident = sb0("ident", [P, P])
        nhalf = sb0("nhalf", [P, 8])
        none_ = sb0("neg_one", [P, 8])
        eps_l = sb0("eps_layer", [P, 8])
        eps_r = sb0("eps_rms", [P, 8])
        small = (nhalf, none_, eps_l, eps_r)
        gate_x = sb0("gate_x", [P, 1])
        gate_f = sb0("gate_f", [P, 1])
        wc = sb0("wc", [P, C, E])
        bcol = sb0("bcol", [P, 1])
        b1c = sb0("b1c", [P, Q])
        b2s = sb0("b2s", [P, D])
        tie = sb0("tie", [P, G])
        gmask = sb0("gmask", [P, GT])
        identb = sb0("identb", [P, P], BF16)
        consts = (wc, bcol, b1c, b2s, tie, gmask, identb)
        const_loads = [(wc, Wc.rearrange("(c p) e s -> p c (e s)", p=P)), (bcol, bc), (b1c, b1),
                       (b2s, b2.rearrange("e s d -> (e s) d")), (tie, tie_in.partition_broadcast(P)), (gmask, gmask_in)]
        attn = ExitStack()
        with attn:
            sba = lambda n, s, dt=F32: attn.enter_context(nc.sbuf_tensor(n, s, dt))
            cos = sba("cos", [P, S + T])
            sin = sba("sin", [P, S + T])
            qh = sba("qh", [P, C, D], F32R)
            ql = sba("ql", [P, C, D], F32R)
            xin = sba("xin", [P, UNITS, TH, D])
            prologue(nc, sem, ps, w1, ident, small, gate_x, gate_f, cos, sin, qh, ql, const_loads, identb, xin, x,
                     ctx_in, mask, gx_in, gf_in, rms, q_w, kv_w, out_w, W1,
                     ident_in, cos_in, sin_in, kr_dram, vw_dram)
            attention(nc, sem, ps, ident, small, cos, sin, qh, ql, xin, w1, W1, x, kr_dram, vw_dram, x1_dram)
        experts(nc, sem, ps, w1, consts, ident, small, gate_f, x1_dram, W2, out)


UNITS = 4


def unit_tokens(d, u):
    return d.rearrange("k (n p) d -> k p n d", p=P)[u // 2][:, (u % 2) * TH:(u % 2 + 1) * TH, :]


def prologue(nc, sem, ps, w1, ident, small, gate_x, gate_f, cos, sin, qh, ql, const_loads, identb, xin, x,
             ctx_in, mask, gx_in, gf_in, rms, q_w, kv_w, out_w, W1,
             ident_in, cos_in, sin_in, kr_dram, vw_dram):
    nhalf, none_, eps_l, eps_r = small
    st = ExitStack()
    with st:
        sb = lambda n, s, dt=F32: st.enter_context(nc.sbuf_tensor(n, s, dt))
        NC = B * S // P
        VB = 4
        cx = sb("cx", [P, NC, D])
        mnT = sb("mnT", [P, C, B * S])
        vT = sb("vT", [P, B * S])
        kr = sb("kr", [P, B, 2 * S + 1])
        kt = sb("kt", [P, 2, HT])
        ow = sb("ow", [P, H, D])
        qraw = sb("qraw", [P, C, H, DH])
        kvraw = sb("kvraw", [P, C, 2 * DH])
        kvs = sb("kvs", [P, C, 3 * DH])
        vwb = cx[:].rearrange("p (b a) d -> p b a d", a=2)
        rs1 = sb("rs1", [P, C])
        mk = sb("mk", [P, B], U8)
        mkf = sb("mkf", [P, B])
        bst = sb("bst", [P, NC, 6])
        mv = sb("mv", [P, NC, 2])
        ms = sb("ms", [P, NC])
        ms2 = sb("ms2", [P, NC])
        rr = sb("rr", [P, NC])
        gts = sb("gts", [P, 2])

        names = [f"ctx{t}" for t in range(0, NC, 2)] + ["small", "qw", "kvw", "ow", "tab", "const", "x"]
        L = {n: sem(f"p_{n}") for n in names}
        s_vws = [sem(f"p_vws{k}") for k in range(VB)]
        s_krs = sem("p_krs")
        count = {}

        cT = [("cT", c, h) for h in range(2) for c in range(C)]
        kj = [("k", w, h) for w in range(2) for h in range(2)]
        vj = [("v", h) for h in range(2)]
        vwj = [("vw", b, pr) for b in range(B) for pr in range(2)]
        pe_names = cT + kj + vj + vwj
        act_names = (["gate"] + [("cn", t) for t in range(NC)] + [("mn",) + n[1:] for n in cT]
                     + [("vT", h) for h in range(2)] + [("vwe", b, pr) for b in range(B) for pr in range(2)])
        rope = [(o, h) for h in range(2) for o in ("kC", "sS", "k0", "sC", "kS", "k1")]
        dve_names = ([(o, t) for h in range(2) for o in ("st", "ag") for t in range(4 * h, 4 * h + 4)] + ["sc1"]
                     + [("qs", c) for c in range(C)] + ["qhi", "qlo"]
                     + [("kvs", c) for c in range(C)] + [("ks1", c) for c in range(C)] + [("ks2", c) for c in range(C)]
                     + ["mkf", "mkb", "idb"] + rope)
        pool_names = ["nh"] + [(f"ms{k}", h) for h in range(2) for k in range(4)]
        PE, AC, DV, PO = (Steps(sem(f"p_{n}s"), l) for n, l in
                          (("pe", pe_names), ("act", act_names), ("dve", dve_names), ("pool", pool_names)))

        blk = st.enter_context(nc.Block())

        @blk.sync
        def _(e):
            def load(name, *pairs):
                for o, s in pairs:
                    e.dma_start(o, s).then_inc(L[name], 16)
                    count[name] = count.get(name, 0) + 16
            for s in (PE, AC, DV, PO):
                e.sem_inc(s.sem, s.per)
            for t in range(0, NC, 2):
                load(f"ctx{t}", (cx[:, t:t + 2], ctx_in.rearrange("b s d -> (b s) d").rearrange("(n p) d -> p n d", p=P)[:, t:t + 2]))
            load("small", (rs1[:], rms),
                 (gts[:, 0:1], gx_in.partition_broadcast(P)), (gts[:, 1:2], gf_in.partition_broadcast(P)),
                 (mk[0:S, :], mask), (mk[S:P, :], mask),
                 (ident[:], ident_in))
            load("kvw", *[(kvraw[:, :, k * DH:(k + 1) * DH], kv_w[k, 0].rearrange("(c p) h -> p c h", p=P)) for k in range(2)])
            load("qw", *[(qraw[:, :, n, :], q_w[n].rearrange("(c p) h -> p c h", p=P)) for n in range(H)])
            load("tab", (cos[:], cos_in), (sin[:], sin_in))
            load("ow", (ow[:], out_w.rearrange("n h d -> h n d")))
            for u in range(UNITS):
                load("x", (xin[:, u], unit_tokens(x[0:2], u)))
            load("const", *[(o[:], v) for o, v in const_loads])

            def store_vw(b):
                e.wait_ge(AC.sem, AC.done(0, ("vwe", b, 1)))
                e.dma_start(vw_dram[b], vwb[:, b % VB]).then_inc(s_vws[b % VB], 16)
            e.wait_ge(DV.sem, DV.done(0, ("k1", 1)))
            e.dma_start(kr_dram.rearrange("b p k -> p b k"), kr[:]).then_inc(s_krs, 16)
            for b in range(B):
                store_vw(b)
            e.wait_ge(L["const"], count["const"])
            e.wait_ge(L["x"], count["x"])
            e.wait_ge(s_krs, 16)
            for s in s_vws:
                e.wait_ge(s, 16 * B // VB)

        def pool_plan():
            def nh(e, i, w):
                for t, v in ((none_, -1.0), (eps_l, LN_EPS), (eps_r, RMS_EPS)):
                    e.memset(t[:], v)
                return e.memset(nhalf[:], -0.5)
            yield "nh", nh

            for h in range(2):
                half = slice(4 * h, 4 * h + 4)
                chain = [(ms[:, half], mv[:, half, 0], mv[:, half, 0], ALU.mult),
                         (ms2[:, half], ms[:, half], mv[:, half, 1], ALU.add),
                         (ms[:, half], ms2[:, half], eps_r[:, 0:4], ALU.add),
                         (rr[:, half], ms[:, half], nhalf[:, 0:4], ALU.pow)]
                for k, ops in enumerate(chain):
                    def m(e, i, w, h=h, k=k, ops=ops):
                        if k:
                            w(PO, (f"ms{k - 1}", h))
                        else:
                            w(DV, ("ag", 4 * h + 3))
                            w(PO, "nh")
                        return e.tensor_tensor(*ops)
                    yield (f"ms{k}", h), m

        @blk.gpsimd
        def _(e):
            run_steps(e, PO, list(pool_plan()))

        def act_plan():
            def gate(e, i, w):
                e.wait_ge(L["small"], count["small"])
                e.activation(gate_x[:], gts[:, 0:1], ACT.Tanh)
                return e.activation(gate_f[:], gts[:, 1:2], ACT.Tanh)
            yield "gate", gate
            for t in range(NC):
                def cn(e, i, w, t=t):
                    w(PO, ("ms3", t // 4))
                    return e.activation(cx[:, t, :], cx[:, t, :], ACT.Copy, scale=rr[:, t:t + 1])
                yield ("cn", t), cn
            for _, c, h in cT:
                def mn(e, i, w, c=c, h=h):
                    w(PE, ("cT", c, h))
                    return e.activation(mnT[:, c, h * HT:(h + 1) * HT], ps[:, 2 * c + h, :], ACT.Copy)
                yield ("mn", c, h), mn
            for h in range(2):
                def v(e, i, w, h=h):
                    w(PE, ("v", h))
                    return e.activation(vT[:, h * HT:(h + 1) * HT], ps[:, 4 + h, :], ACT.Copy)
                yield ("vT", h), v
            for b in range(B):
                for pr in range(2):
                    def vwe(e, i, w, b=b, pr=pr):
                        w(PE, ("vw", b, pr))
                        if b >= VB and pr == 0:
                            e.wait_ge(s_vws[b % VB], 16 * (b // VB))
                        if b == 0:
                            w(AC, "gate")
                        return e.activation(vwb[:, b % VB, pr, :], ps[:, 4 + 2 * (b % 2) + pr, :], ACT.Copy, scale=gate_x[:])
                    yield ("vwe", b, pr), vwe

        @blk.scalar
        def _(e):
            run_steps(e, AC, list(act_plan()))

        def dve_plan():
            for h in range(2):
                for t in range(4 * h, 4 * h + 4):
                    def s_(e, i, w, t=t):
                        e.wait_ge(L[f"ctx{t - t % 2}"], 16)
                        return e.bn_stats(bst[:, t, :], cx[:, t, :])
                    yield ("st", t), s_
                for t in range(4 * h, 4 * h + 4):
                    def a_(e, i, w, t=t):
                        w(DV, ("st", t))
                        return e.bn_aggr(mv[:, t, :], bst[:, t, :])
                    yield ("ag", t), a_

            def sc1(e, i, w):
                e.wait_ge(L["small"], count["small"])
                return e.tensor_scalar(rs1[:], rs1[:], 1.0, None, ALU.add)
            yield "sc1", sc1
            for c in range(C):
                def qs(e, i, w, c=c):
                    e.wait_ge(L["qw"], count["qw"])
                    w(DV, "sc1")
                    v = qraw[:, c].rearrange("p n h -> p (n h)")
                    return e.tensor_scalar(v, v, rs1[:, c:c + 1], None, ALU.mult)
                yield ("qs", c), qs
            qf = qraw[:].rearrange("p c n h -> p (c n h)")

            def qhi(e, i, w):
                w(DV, ("qs", C - 1))
                return e.tensor_copy(qh[:].rearrange("p c n -> p (c n)"), qf)
            yield "qhi", qhi

            def qlo(e, i, w):
                w(DV, "qhi")
                return e.tensor_tensor(ql[:].rearrange("p c n -> p (c n)"), qf,
                                       qh[:].rearrange("p c n -> p (c n)").bitcast(F32), ALU.subtract)
            yield "qlo", qlo
            for c in range(C):
                def kv(e, i, w, c=c):
                    e.wait_ge(L["kvw"], count["kvw"])
                    return e.tensor_scalar(kvs[:, c, 0:2 * DH], kvraw[:, c, :], rs1[:, c:c + 1], None, ALU.mult)
                yield ("kvs", c), kv
            HH = DH // 2
            for k in range(2):
                for c in range(C):
                    def ks(e, i, w, c=c, k=k):
                        return e.tensor_scalar(kvs[:, c, 2 * DH + k * HH:2 * DH + (k + 1) * HH],
                                               kvraw[:, c, (1 - k) * HH:(2 - k) * HH], rs1[:, c:c + 1], None, ALU.mult)
                    yield (f"ks{k + 1}", c), ks
            yield "mkf", lambda e, i, w: e.tensor_copy(mkf[:], mk[:])

            def mkb(e, i, w):
                w(DV, "mkf")
                return e.tensor_scalar(kr[:, :, 2 * S], mkf[:], -FILL, FILL, ALU.mult, ALU.add)
            yield "mkb", mkb
            yield "idb", lambda e, i, w: e.tensor_copy(identb[:], ident[:])
            nb = HT // S
            for h in range(2):
                def tab(t):
                    return t[:, 0:S].unsqueeze(1).broadcast_to([P, nb, S])
                def krv(k):
                    return kr[:, h * nb:(h + 1) * nb, k * S:(k + 1) * S]
                def psv(w_, h=h):
                    return ps[:, 2 * w_ + h, :].rearrange("p (b s) -> p b s", s=S)
                kv0 = kt[:, 0, :].rearrange("p (b s) -> p b s", s=S)
                kv1 = kt[:, 1, :].rearrange("p (b s) -> p b s", s=S)
                k0v, k1v = krv(0), krv(1)

                def f1(e, i, w, h=h, o=kv0, a=psv(0), t=tab(cos)):
                    w(PE, ("k", 1, h))
                    e.wait_ge(L["tab"], count["tab"])
                    if h:
                        w(DV, ("k1", h - 1))
                    return e.tensor_tensor(o, a, t, ALU.mult)
                yield ("kC", h), f1
                yield ("sS", h), lambda e, i, w, h=h, o=kv1, a=psv(1), t=tab(sin): e.tensor_tensor(o, a, t, ALU.mult)

                def f3(e, i, w, h=h, o=k0v, a=kv0, b=kv1):
                    w(DV, ("sS", h))
                    return e.tensor_tensor(o, a, b, ALU.subtract)
                yield ("k0", h), f3

                def f4(e, i, w, h=h, o=kv0, a=psv(1), t=tab(cos)):
                    w(DV, ("k0", h))
                    return e.tensor_tensor(o, a, t, ALU.mult)
                yield ("sC", h), f4
                yield ("kS", h), lambda e, i, w, h=h, o=kv1, a=psv(0), t=tab(sin): e.tensor_tensor(o, a, t, ALU.mult)

                def f6(e, i, w, h=h, o=k1v, a=kv0, b=kv1):
                    w(DV, ("kS", h))
                    return e.tensor_tensor(o, a, b, ALU.add)
                yield ("k1", h), f6

        @blk.vector
        def _(e):
            run_steps(e, DV, list(dve_plan()))

        def pe_plan():
            for _, c, h in cT:
                def f(e, i, w, c=c, h=h):
                    e.wait_ge(L["small"], count["small"])
                    w(AC, ("cn", 4 * h + 3))
                    for t in range(4):
                        last = e.transpose(ps[:, 2 * c + h, t * P:(t + 1) * P], cx[:, 4 * h + t, c * P:(c + 1) * P], ident[:])
                    return last
                yield ("cT", c, h), f
            for _, k, h in kj:
                def f(e, i, w, k=k, h=h):
                    w(AC, ("mn", C - 1, 1)); w(DV, ("ks2", C - 1))
                    for c in range(C):
                        last = e.matmul(ps[:, 2 * k + h, :], kvs[:, c, 2 * DH * k:2 * DH * k + DH],
                                        mnT[:, c, h * HT:(h + 1) * HT], start=(c == 0), stop=(c == C - 1))
                    return last
                yield ("k", k, h), f
            for _, h in vj:
                def f(e, i, w, h=h):
                    for c in range(C):
                        last = e.matmul(ps[:, 4 + h, :], kvs[:, c, DH:2 * DH],
                                        mnT[:, c, h * HT:(h + 1) * HT], start=(c == 0), stop=(c == C - 1))
                    return last
                yield ("v", h), f
            for _, b, pr in vwj:
                def f(e, i, w, b=b, pr=pr):
                    e.wait_ge(L["ow"], count["ow"])
                    w(AC, ("vwe", b - 2, pr) if b >= 2 else ("vT", 1))
                    for n in range(2):
                        last = e.matmul(ps[n * S:(n + 1) * S, 4 + 2 * (b % 2) + pr, :], vT[:, b * S:(b + 1) * S], ow[:, 2 * pr + n, :],
                                        start=True, stop=True)
                    return last
                yield ("vw", b, pr), f

        @blk.tensor
        def _(e):
            run_steps(e, PE, list(pe_plan()))




def attention(nc, sem, ps, ident, small, cos, sin, qh, ql, xin, w1, w1_dram, x, kr_dram, vw_dram, x1_dram):
    nhalf, none_, eps_l, eps_r = small
    st = ExitStack()
    with st:
        sb = lambda n, s, dt=F32: st.enter_context(nc.sbuf_tensor(n, s, dt))
        xh = sb("xh", [P, TH, D])
        xTh = sb("xTh", [P, C, HT], F32R)
        xTl = sb("xTl", [P, C, HT], F32R)
        qc = sb("qc", [P, H, HT])
        qs = sb("qs", [P, H, HT])
        lt = sb("lt", [P, 2, HT])
        lg = sb("lg", [P, 2, 512])
        pr_ = sb("pr", [P, 2, 512])
        pTh = sb("pTh", [P, 2, 512], F32R)
        pTl = sb("pTl", [P, 2, 512], F32R)
        kb = sb("kb", [P, 2, 2 * S + 1])
        vraw = sb("vraw", [P, 2, D])
        vw = sb("vw", [P, 2, 2, 2, D], F32R)
        bst = sb("a_bst", [P, 2, TH, 6])
        mv = sb("a_mv", [P, UNITS, TH, 2])
        va, r1, vb, vc, r2, sc, nb = (sb(n, [P, UNITS, TH]) for n in ("va", "r1", "vb", "vc", "r2", "sc", "nb"))
        mx = sb("mx", [P, 2, 8])
        sm = sb("sm", [P, 2, 8])
        rc = sb("rc", [P, 2, 8])
        junk = sb("a_junk", [P, 1])

        stat_steps = ("st", "ag", "va", "r1", "vb", "vc", "vd", "r2", "sc", "ns", "nb")
        norm_steps = ("xh", "T", "hi", "lo")
        query_steps = ("Q", "qc", "qs", "L", "lt")

        def lead(n):
            u = n[1]
            return (n[0] == "x" or n[0] in stat_steps and u < 3 or n[0] in norm_steps and u < 2
                    or n[0] in query_steps and u < 1 or n[0] in ("kb", "vw", "vh", "vl", "w1") and u == 0)

        def at(wait):
            def f(who, what, *_):
                u = what[1]
                wait(who, (what[0], u % UNITS) + what[2:], -(u // UNITS))
            return f

        def pair(i):
            return slice(i, i + 1) if isinstance(i, int) else bass.ds(i, 1)

        def scratch(d, i, k):
            return d.rearrange("(r k) p n -> r k p n", k=2)[pair(i), k].rearrange("o p n -> (o p) n")

        pe, act, dve, pool, sync = {}, {}, {}, {}, {}
        for u in range(UNITS):
            def f(e, i, w, u=u):
                w(f"o{u}", ("xo", u), 1)
                return e.dma_start(xin[:, u], unit_tokens(x.rearrange("(r k) t d -> r k t d", k=2)[pair(i)].rearrange("o k t d -> (o k) t d"), u))
            sync["x", u] = f

            def f(e, i, w, u=u):
                w("dve", ("rs", u, TH - 1))
                return e.dma_start(unit_tokens(x1_dram[2 * i:2 * i + 2] if isinstance(i, int) else x1_dram[bass.ds(2 * i, 2)], u), xin[:, u])
            sync["xo", u] = f

            for t in range(TH):
                def f(e, i, w, u=u, t=t):
                    w(f"x{u}", ("x", u))
                    return e.bn_stats(bst[:, u % 2, t, :], xin[:, u, t, :])
                dve["st", u, t] = f

                def f(e, i, w, u=u, t=t):
                    if t == 0:
                        w("pool", ("nb", u), 1)
                        w("dve", ("st", u, TH - 1))
                        e.memset(junk[:], 0.0)
                    return e.bn_aggr(mv[:, u, t, :], bst[:, u % 2, t, :])
                dve["ag", u, t] = f

            var, mean = mv[:, u, :, 1], mv[:, u, :, 0]
            chain = [
                ("va", va[:, u], var, eps_l[:, 0:TH], ALU.add),
                ("r1", r1[:, u], va[:, u], nhalf[:, 0:TH], ALU.pow),
                ("vb", vb[:, u], var, r1[:, u], ALU.mult),
                ("vc", vc[:, u], vb[:, u], r1[:, u], ALU.mult),
                ("vd", vb[:, u], vc[:, u], eps_r[:, 0:TH], ALU.add),
                ("r2", r2[:, u], vb[:, u], nhalf[:, 0:TH], ALU.pow),
                ("sc", sc[:, u], r1[:, u], r2[:, u], ALU.mult),
                ("ns", vc[:, u], sc[:, u], none_[:, 0:TH], ALU.mult),
                ("nb", nb[:, u], mean, vc[:, u], ALU.mult),
            ]
            for k, (o, *ops) in enumerate(chain):
                def f(e, i, w, u=u, k=k, ops=ops, chain=chain):
                    if k:
                        w("pool", (chain[k - 1][0], u))
                    else:
                        w("dve", ("ag", u, TH - 1))
                        w("act", ("xh", u, TH - 1), 1)
                    return e.tensor_tensor(*ops)
                pool[o, u] = f
            norm_chain = [o for o, *_ in chain]

            for t in range(TH):
                def f(e, i, w, u=u, t=t):
                    w("pool", ("nb", u))
                    at(w)("pe", ("T", u - 1, C - 1))
                    return e.activation(xh[:, t, :], xin[:, u, t, :], ACT.Identity,
                                        scale=sc[:, u, t:t + 1], bias=nb[:, u, t:t + 1])
                act["xh", u, t] = f
            for c in range(C):
                def f(e, i, w, u=u, c=c):
                    w("act", ("xh", u, TH - 1))
                    at(w)("dve", ("lo", u, c - 2) if c >= 2 else ("rs", u - 3, 2 + c))
                    for t in range(TH):
                        last = e.transpose(ps[:, c % 2, t * P:(t + 1) * P], xh[:, t, c * P:(c + 1) * P], ident[:])
                    return last
                pe["T", u, c] = f

                def f(e, i, w, u=u, c=c):
                    w("pe", ("T", u, c))
                    return e.activation(xTh[:, c, :], ps[:, c % 2, :], ACT.Copy)
                act["hi", u, c] = f

                def f(e, i, w, u=u, c=c):
                    w("act", ("hi", u, c))
                    return e.tensor_tensor(xTl[:, c, :], ps[:, c % 2, :], xTh[:, c, :].bitcast(F32), ALU.subtract)
                dve["lo", u, c] = f
            for n in range(H):
                def f(e, i, w, u=u, n=n):
                    if n >= 2:
                        w("dve", ("qs", u, n - 2))
                    else:
                        w("dve", ("lo", u, C - 1))
                        at(w)("dve", ("qs", u - 1, n + 2))
                    parts = [(a, b, c) for c in range(C) for a, b in ((qh, xTh), (qh, xTl), (ql, xTh))]
                    for k, (a, b, c) in enumerate(parts):
                        last = e.matmul(ps[:, 2 + n % 2, :], a[:, c, n * DH:(n + 1) * DH], b[:, c, :],
                                        start=(k == 0), stop=(k == len(parts) - 1))
                    return last
                pe["Q", u, n] = f
                for o, tab, dst in (("qc", cos, qc), ("qs", sin, qs)):
                    def f(e, i, w, u=u, n=n, tab=tab, dst=dst):
                        w("pe", ("Q", u, n))
                        h = u % 2
                        return e.tensor_tensor(dst[:, n, :], ps[:, 2 + n % 2, :],
                                               tab[:, S + h * HT:S + (h + 1) * HT], ALU.mult)
                    dve[o, u, n] = f
            for p in range(2):
                def f(e, i, w, u=u, p=p):
                    w("dve", ("qs", u, 2 * p + 1))
                    at(w)("act", ("lt", u if p else u - 1, 1 - p))
                    w(f"k{u // 2}", ("kb", u // 2))
                    for k in range(2):
                        for n in range(2):
                            last = e.matmul(ps[n * S:(n + 1) * S, 4, :], kb[:, u // 2, k * S:(k + 1) * S],
                                            (qc, qs)[k][:, 2 * p + n, :], start=(k == 0), stop=(k == 1))
                    return last
                pe["L", u, p] = f

                def f(e, i, w, u=u, p=p):
                    w("pe", ("L", u, p))
                    return e.activation(lt[:, p, :], ps[:, 4, :], ACT.Identity,
                                        scale=float(DH) ** -0.5, bias=kb[:, u // 2, 2 * S:2 * S + 1])
                act["lt", u, p] = f

            def heads(v):
                return v.rearrange("p (a s) -> p a s", s=S)
            for tp in range(2):
                def f(e, i, w, u=u, tp=tp):
                    w("act", ("lt", u, 1))
                    at(w)("dve", ("sb", u - 1, tp))
                    for t in range(2):
                        for p in range(2):
                            last = e.transpose(ps[:, 5 + tp, (2 * t + p) * P:(2 * t + p + 1) * P],
                                               lt[:, p, (2 * tp + t) * P:(2 * tp + t + 1) * P], ident[:])
                    return last
                pe["LT", u, tp] = f

                def f(e, i, w, u=u, tp=tp):
                    w("pe", ("LT", u, tp))
                    return e.tensor_reduce(out=mx[:, tp, :], in_=heads(ps[:, 5 + tp, :]), op=ALU.max, axis=AX_X)
                dve["mx", u, tp] = f

                def f(e, i, w, u=u, tp=tp):
                    w("dve", ("mx", u, tp))
                    at(w)("pool", ("pr", u - 1, tp))
                    return e.tensor_tensor(heads(lg[:, tp, :]), heads(ps[:, 5 + tp, :]),
                                           mx[:, tp, :].unsqueeze(2).broadcast_to([P, 8, S]), ALU.subtract)
                dve["sb", u, tp] = f

                def f(e, i, w, u=u, tp=tp):
                    w("dve", ("sb", u, tp))
                    return e.activation(lg[:, tp, :], lg[:, tp, :], ACT.Exp)
                act["ex", u, tp] = f

                def f(e, i, w, u=u, tp=tp):
                    w("act", ("ex", u, tp))
                    return e.tensor_reduce(out=sm[:, tp, :], in_=heads(lg[:, tp, :]), op=ALU.add, axis=AX_X)
                dve["sm", u, tp] = f

                def f(e, i, w, u=u, tp=tp):
                    w("dve", ("sm", u, tp))
                    return e.reciprocal(rc[:, tp, :], sm[:, tp, :])
                dve["rc", u, tp] = f

                def f(e, i, w, u=u, tp=tp):
                    w("dve", ("rc", u, tp))
                    at(w)("pe", ("PT", u - 1, tp))
                    return e.tensor_tensor(heads(pr_[:, tp, :]), heads(lg[:, tp, :]),
                                           rc[:, tp, :].unsqueeze(2).broadcast_to([P, 8, S]), ALU.mult)
                pool["pr", u, tp] = f

                def f(e, i, w, u=u, tp=tp):
                    w("pool", ("pr", u, tp))
                    at(w)("dve", ("pl", u if tp else u - 1, 1 - tp))
                    for k in range(4):
                        last = e.transpose(ps[:, 7, k * P:(k + 1) * P], pr_[:, tp, k * P:(k + 1) * P], ident[:])
                    return last
                pe["PT", u, tp] = f

                def f(e, i, w, u=u, tp=tp):
                    w("pe", ("PT", u, tp))
                    return e.activation(pTh[:, tp, :], ps[:, 7, :], ACT.Copy)
                act["pT", u, tp] = f

                def f(e, i, w, u=u, tp=tp):
                    w("act", ("pT", u, tp))
                    return e.tensor_tensor(pTl[:, tp, :], ps[:, 7, :], pTh[:, tp, :].bitcast(F32), ALU.subtract)
                dve["pl", u, tp] = f
            for t in range(TH):
                def f(e, i, w, u=u, t=t):
                    at(w)("dve", ("rs", u, t - 2) if t >= 2 else ("lo", u + 2, 2 + t))
                    w("dve", ("pl", u, t // 2))
                    w("dve", ("vl", u // 2))
                    parts = [(a, k, p) for p in range(2) for a, k in ((pTh, 0), (pTh, 1), (pTl, 0))]
                    for m, (a, k, p) in enumerate(parts):
                        column = (2 * (t % 2) + p) * P
                        last = e.matmul(ps[:, t % 2, :], a[:, t // 2, column:column + P], vw[:, u // 2, k, p, :],
                                        start=(m == 0), stop=(m == len(parts) - 1))
                    return last
                pe["PV", u, t] = f

                def f(e, i, w, u=u, t=t):
                    w("pe", ("PV", u, t))
                    return e.tensor_tensor(xin[:, u, t, :], ps[:, t % 2, :], xin[:, u, t, :], ALU.add)
                dve["rs", u, t] = f
        def load_w1(e, i, w):
            part = C * E * F // (B // 2)
            v = slice(i * part, (i + 1) * part) if isinstance(i, int) else bass.ds(i * part, part)
            return e.dma_start(w1[:].rearrange("p c n -> p (c n)")[:, v], w1_dram.rearrange("p c n -> p (c n)")[:, v])
        sync["w1", 0] = load_w1

        for k in range(2):
            def f(e, i, w, k=k):
                w("act", ("lt", 2 * k + 1, 1), 1)
                return e.dma_start(kb[:, k], scratch(kr_dram, i, k))
            sync["kb", k] = f

            def f(e, i, w, k=k):
                w("dve", ("vl", 1 - k), int(k == 0))
                return e.dma_start(vraw[:].rearrange("p a d -> p (a d)"), scratch(vw_dram.rearrange("b p a d -> b p (a d)"), i, k))
            sync["vw", k] = f

            def f(e, i, w, k=k):
                w(f"v{k}", ("vw", k))
                w("pe", ("PV", 2 * k + 1, TH - 1), 1)
                return e.activation(vw[:, k, 0], vraw[:], ACT.Copy)
            act["vh", k] = f

            def f(e, i, w, k=k):
                w("act", ("vh", k))
                return e.tensor_tensor(vw[:, k, 1], vraw[:], vw[:, k, 0].bitcast(F32), ALU.subtract)
            dve["vl", k] = f

        def order(parts):
            out = []
            for u in range(UNITS):
                for p in parts:
                    out.append((p[0], (u + p[1]) % UNITS) + tuple(p[2:]))
            return out

        pe_order = order([("LT", 0, 0), ("LT", 0, 1)] + [("Q", 1, n) for n in range(H)]
                         + [("T", 2, 0), ("T", 2, 1), ("L", 1, 0), ("PT", 0, 0), ("T", 2, 2), ("T", 2, 3), ("L", 1, 1), ("PT", 0, 1)]
                         + [("PV", 0, t) for t in range(TH)])
        act_order = order([("ex", 0, 0), ("ex", 0, 1)] + [("xh", 2, t) for t in range(TH)] + [("hi", 2, 0), ("hi", 2, 1)]
                          + [("lt", 1, 0), ("pT", 0, 0), ("hi", 2, 2), ("hi", 2, 3), ("lt", 1, 1), ("pT", 0, 1)])
        dve_order = order([("mx", 0, 0), ("sb", 0, 0), ("mx", 0, 1), ("sb", 0, 1), ("qc", 1, 0), ("qs", 1, 0),
                           ("sm", 0, 0), ("rc", 0, 0), ("sm", 0, 1), ("rc", 0, 1), ("qc", 1, 1), ("qs", 1, 1),
                           ("qc", 1, 2), ("qs", 1, 2), ("st", 3, 0), ("st", 3, 1), ("qc", 1, 3), ("qs", 1, 3)]
                          + [("lo", 2, 0), ("lo", 2, 1), ("pl", 0, 0), ("lo", 2, 2), ("lo", 2, 3)]
                          + [("st", 3, 2), ("pl", 0, 1), ("rs", 0, 0), ("st", 3, 3), ("rs", 0, 1)]
                          + [("ag", 3, t) for t in range(TH)] + [("rs", 0, 2), ("rs", 0, 3)])
        for k, u in ((1, 1), (0, 3)):
            act_order.insert(act_order.index(("hi", (u + 2) % UNITS, 0)), ("vh", k))
            dve_order.insert(dve_order.index(("st", (u + 3) % UNITS, 0)), ("vl", k))
        pool_order = order([("pr", 0, 0), ("pr", 0, 1)] + [(o, 3) for o in norm_chain])
        sync_order = []
        for u in range(UNITS):
            sync_order += {0: [("kb", 1), ("vw", 1)], 2: [("kb", 0), ("vw", 0)]}.get(u, [])
            sync_order += [("xo", u), ("x", u)]
        sync_order.append(("w1", 0))
        plans = {"pe": (pe, pe_order), "act": (act, act_order), "dve": (dve, dve_order), "pool": (pool, pool_order),
                 "sync": (sync, sync_order)}
        slots = {f"x{u}": [("x", u)] for u in range(UNITS)}
        slots |= {f"k{k}": [("kb", k)] for k in range(2)} | {f"v{k}": [("vw", k)] for k in range(2)}
        slots["w1"] = [("w1", 0)]
        slots |= {f"o{u}": [("xo", u)] for u in range(UNITS)}
        Phase(nc, sem, "a", {k: [(n, d[n]) for n in o] for k, (d, o) in plans.items()}, slots, lead, B // 2, ("x",))


def experts(nc, sem, ps, w1, consts, ident, small, gate_f, x1_dram, w2_dram, out):
    nhalf, none_, eps_l, eps_r = small
    st = ExitStack()
    with st:
        sb = lambda n, s, dt=F32: st.enter_context(nc.sbuf_tensor(n, s, dt))
        QH = Q // 2
        GB = NT // 2
        NB = Q // QB
        wc, bcol, b1c, b2s, tie, gmask, identb = consts
        w2s = sb("w2s", [P, 4, QB * P])
        xin = sb("b_xin", [P, 4, D])
        xf = sb("xf", [P, 2, D])
        xnh = sb("xnh", [P, NT, D], F32R)
        xnl = sb("xnl", [P, NT, D], F32R)
        gat = sb("gat", [P, 2, QH * 4 * NG])
        xT = gat[:].rearrange("p h (c t) -> p h c t", t=HT)
        lgt = sb("lgt", [P, HT])
        hb = lgt
        top_ = sb("top", [P, HT // G])
        selT = sb("selT", [P, T])
        selN = sb("selN", [P, T], BF16)
        sel = sb("sel", [P, NT, P], BF16)
        selb = sb("selb", [P, NT, QH * 4 * GT], F32R)
        hid = sb("hid", [P, Q, 4 * NG])
        res = sb("res", [P, 2, Q * P])
        y = sb("y", [P, 2, 4, P])
        bst = sb("b_bst", [P, NT, 6])
        mv = sb("b_mv", [P, NT, 2])
        va, r1, ns, nb = (sb(n, [P, NT // 2, 2]) for n in ("b_va", "b_r1", "b_ns", "b_nb"))
        junk = sb("b_junk", [P, 1])

        s_m = sem("b_set")
        with nc.Block() as blk:
            @blk.vector
            def _(e):
                e.memset(hid[:, 0:Q // 2], 0.0).then_inc(s_m, 1)

            @blk.gpsimd
            def _(e):
                e.memset(hid[:, Q // 2:Q], 0.0).then_inc(s_m, 1)

        rooms = {"res0": res[:, 1, 0:4 * QB * P], "res1": res[:, 1, 4 * QB * P:8 * QB * P],
                 "half0": gat[:, 0, :], "half1": gat[:, 1, :]}
        kinds = ["own", "res0", "res1", "own", "half0", "own", "half1", "own"]

        def piece(n):
            kind, k = kinds[n // 4], n % 4
            if kind == "own":
                return ("w2", n), w2s[:, k, :]
            return ("w2", n - k), rooms[kind][:, k * QB * P:(k + 1) * QB * P]

        def slot(n):
            return f"w_{kinds[n // 4]}" + (str(n % 4) if kinds[n // 4] == "own" else "")

        loads = sorted({piece(n)[0][1] for n in range(NB * C)})

        AHEAD = [("ga", 0, 0), ("ga", 0, 1)]
        LEAD = {"x", "st", "ag", "va", "r1", "ns", "nb", "lo", "xf", "hi", "T", "xT", "lg", "mx", "eq", "sT", "sel"}

        def lead(n):
            return n[0] in LEAD or n[0] == "sp" and n[1] == 0 or n[:3] in AHEAD

        def batch(d, i, t0, n):
            d = d[i:i + 1] if isinstance(i, int) else d[bass.ds(i, 1)]
            return d.rearrange("o (n p) d -> p (o n) d", p=P)[:, t0:t0 + n, :]

        front = ([("T", t) for t in range(4)] + [("lg", 0)] + [("T", t) for t in range(4, 8)]
                 + [("lg", 1), ("sT", 0), ("sT", 1)])
        reader = {"T": ("act", "xT"), "lg": ("dve", "lg"), "sT": ("act", "sel")}
        front_bank = {n: 2 + k % 2 for k, n in enumerate(front)}

        def bank_read(w, n):
            k = front.index(n)
            if k >= 2:
                eng, o = reader[front[k - 2][0]]
                return w(eng, (o, front[k - 2][1]))
            return w("dve", ("hr", 1, 2 + k), 1)

        def sbank(c, h):
            return h + 2 * (c == C - 1)

        def reader_of(eh, c, k):
            return "dve" if k % 2 and ("ga", eh, c) not in AHEAD else "act"

        def normed(t):
            return "xf" if t in (2, 3) else "hi"

        pe, act, dve, pool, sync = {}, {}, {}, {}, {}
        for t in range(NT):
            def f(e, i, w, t=t):
                w("act", (normed(t - 4), (t - 4) % NT), int(t < 4))
                return e.dma_start(xin[:, t % 4, :], batch(x1_dram, i, t, 1)[:, 0])
            sync["x", t] = f

            def f(e, i, w, t=t):
                w(f"x{t % 4}", ("x", t))
                return e.bn_stats(bst[:, t, :], xin[:, t % 4, :])
            dve["st", t] = f

            def f(e, i, w, t=t):
                if t % 2 == 0:
                    w("pool", ("nb", t // 2), 1)
                    w("dve", ("st", t + 1))
                    e.memset(junk[:], 0.0)
                return e.bn_aggr(mv[:, t, :], bst[:, t, :])
            dve["ag", t] = f

            def f(e, i, w, t=t, k=t // 2, j=t % 2):
                w("pool", ("lo", t - 2) if t >= 2 else ("nb", k))
                w("pool", ("nb", k))
                w("pe", ("T", (t - 2) % NT), int(t < 2))
                if t < 2:
                    w("pool", ("lo", t - 2 + NT), 1)
                return e.activation(xf[:, j, :], xin[:, t % 4, :], ACT.Identity, scale=r1[:, k, j:j + 1], bias=nb[:, k, j:j + 1])
            act["xf", t] = f

            def f(e, i, w, t=t, k=t // 2, j=t % 2):
                w("pe", ("ga", 1, C - 1, GB - 1), 1)
                w("pool", ("nb", k))
                return e.activation(xnh[:, t, :], xin[:, t % 4, :], ACT.Identity, scale=r1[:, k, j:j + 1], bias=nb[:, k, j:j + 1])
            act["hi", t] = f

            def f(e, i, w, t=t):
                w("act", (normed(t), t))
                return e.tensor_tensor(xnl[:, t, :], xf[:, t % 2, :], xnh[:, t, :].bitcast(F32), ALU.subtract)
            pool["lo", t] = f

            def f(e, i, w, t=t):
                n = ("T", t)
                if t == TH:
                    bank_read(w, n)
                w("act", ("xf", t))
                bank_read(w, n)
                for c in range(C):
                    last = e.transpose(ps[:, front_bank[n], c * P:(c + 1) * P], xf[:, t % 2, c * P:(c + 1) * P], ident[:])
                return last
            pe["T", t] = f

            def f(e, i, w, t=t):
                w("pe", ("T", t))
                return e.activation(xT[:, t // TH, :, (t % TH) * P:(t % TH + 1) * P],
                                    ps[:, front_bank["T", t], :].rearrange("p (c t) -> p c t", t=P), ACT.Copy)
            act["xT", t] = f
        for k in range(NT // 2):
            var, mean = mv[:, 2 * k:2 * k + 2, 1], mv[:, 2 * k:2 * k + 2, 0]
            chain = [("va", va[:, k], var, eps_l[:, 0:2], ALU.add), ("r1", r1[:, k], va[:, k], nhalf[:, 0:2], ALU.pow),
                     ("ns", ns[:, k], r1[:, k], none_[:, 0:2], ALU.mult), ("nb", nb[:, k], mean, ns[:, k], ALU.mult)]
            for m, (o, *ops) in enumerate(chain):
                def f(e, i, w, k=k, m=m, ops=ops, chain=chain):
                    if m:
                        w("pool", (chain[m - 1][0], k))
                    else:
                        w("dve", ("ag", 2 * k + 1))
                        w("act", (normed(2 * k + 1), 2 * k + 1), 1)
                    return e.tensor_tensor(*ops)
                pool[o, k] = f
        for h in range(2):
            def groups(v):
                return v.rearrange("p (n t) -> p n t", t=G)

            def f(e, i, w, h=h):
                w("act", ("xT", h * TH + TH - 1))
                bank_read(w, ("lg", h))
                for c in range(C):
                    last = e.matmul(ps[:, front_bank["lg", h], :], wc[:, c, :], xT[:, h, c, :], start=(c == 0), stop=(c == C - 1))
                return last
            pe["lg", h] = f

            def f(e, i, w, h=h):
                w("pe", ("lg", h))
                w("dve", ("eq", 0) if h else ("hr", 1, 3), 0 if h else 1)
                return e.scalar_tensor_tensor(out=groups(lgt[:]), in0=groups(ps[:, front_bank["lg", h], :]), scalar=bcol[:],
                                              in1=tie[:].unsqueeze(1).broadcast_to([P, HT // G, G]), op0=ALU.add, op1=ALU.add)
            dve["lg", h] = f

            def f(e, i, w, h=h):
                w("dve", ("lg", h))
                return e.tensor_reduce(out=top_[:], in_=groups(lgt[:]), op=ALU.max, axis=AX_X)
            dve["mx", h] = f

            def f(e, i, w, h=h):
                w("dve", ("mx", h))
                w("act", ("cp", h), 1)
                return e.tensor_tensor(groups(selN[:, h * HT:(h + 1) * HT]), groups(lgt[:]),
                                       top_[:].unsqueeze(2).broadcast_to([P, HT // G, G]), ALU.is_equal)
            dve["eq", h] = f

            def f(e, i, w, h=h):
                w("pe", ("sc", C - 1, 1), 1)
                w("dve", ("eq", h))
                return e.activation(selT[:, h * HT:(h + 1) * HT], selN[:, h * HT:(h + 1) * HT], ACT.Copy)
            act["cp", h] = f

            def f(e, i, w, h=h):
                w("dve", ("eq", h))
                bank_read(w, ("sT", h))
                b = ps[:, front_bank["sT", h], :].bitcast(BF16)
                for t in range(TH):
                    last = e.transpose(b[:, t * P:(t + 1) * P], selN[:, (h * TH + t) * P:(h * TH + t + 1) * P], identb[:])
                return last
            pe["sT", h] = f

            def f(e, i, w, h=h):
                w("pe", ("sT", h))
                w("pool", ("sp", 1, NT - 1), 1)
                b = ps[:, front_bank["sT", h], :].bitcast(BF16)[:, 0:HT]
                return e.activation(sel[:, h * TH:(h + 1) * TH, :].rearrange("p t e -> p (t e)"), b, ACT.Copy)
            act["sel", h] = f
        for eh in range(2):
            for t in range(NT):
                def f(e, i, w, eh=eh, t=t):
                    w("act", ("sel", t // TH))
                    w("pe", ("ga", 1 - eh, C - 1, t // 2), 1 - eh)
                    v = sel[:, t, :].rearrange("p (j q) -> p q j", q=Q)[:, eh * QH:(eh + 1) * QH, :]
                    return e.tensor_tensor(selb[:, t, :].rearrange("p (q j g) -> p q j g", j=4, g=GT),
                                           v.unsqueeze(3).broadcast_to([P, QH, 4, GT]),
                                           gmask[:].unsqueeze(1).unsqueeze(1).broadcast_to([P, QH, 4, GT]), ALU.mult)
                pool["sp", eh, t] = f
            for c in range(C):
                for k in range(GB):
                    who = reader_of(eh, c, k)

                    def f(e, i, w, eh=eh, c=c, k=k, who=who):
                        w("pool", ("sp", eh, 2 * k + 1))
                        if eh == 0 and c == 0:
                            w("pool", ("lo", NT - 1))
                            w("act", ("rs", C - 1, 4 + k), 1)
                        else:
                            m = (eh, c - 1, k) if c else (0, C - 1, k)
                            w(reader_of(*m), ("ga",) + m)
                        for t in range(2):
                            for m, part in enumerate((xnh, xnl)):
                                last = e.matmul(ps[:, 4 + k, t * 256:(t + 1) * 256], part[:, 2 * k + t, c * P:(c + 1) * P],
                                                selb[:, 2 * k + t, :], start=(m == 0), stop=(m == 1))
                        return last
                    pe["ga", eh, c, k] = f

                    def f(e, i, w, eh=eh, c=c, k=k, who=who):
                        w("pe", ("ga", eh, c, k))
                        if c >= 2 or eh:
                            w("pe", ("w1", eh, c - 2, 3) if c >= 2 else ("w1", 0, c + 2, 3))
                        dst = gat[:, c % 2, :].rearrange("p (qj t g) -> p t qj g", t=NT, g=GT)[:, 2 * k:2 * k + 2]
                        src = ps[:, 4 + k, :].rearrange("p (t qj g) -> p t qj g", t=2, g=GT)
                        return e.tensor_copy(dst, src) if who == "dve" else e.activation(dst, src, ACT.Copy)
                    (dve if who == "dve" else act)["ga", eh, c, k] = f

                for b in range(4):
                    def f(e, i, w, eh=eh, c=c, b=b):
                        if c == 0 and eh:
                            w("dve", ("hb", 0, b))
                        elif c == 0:
                            w("dve", ("fin", C - 2 + b // 2, b % 2), 1)
                        if c or eh:
                            w(reader_of(eh, c, GB - 1), ("ga", eh, c, GB - 1))
                            w("act", ("ga", eh, c, GB - 2))
                        else:
                            w("act", ("ga", eh, c, GB - 1))
                        for q in range(QB * b, QB * (b + 1)):
                            last = e.matmul(ps[:, b, (q % QB) * P:(q % QB + 1) * P],
                                            w1[:, c, (eh * QH + q) * P:(eh * QH + q + 1) * P], gat[:, c % 2, q * P:(q + 1) * P],
                                            start=(c == 0 and q % QB == 0), stop=(c == C - 1), skip_group_check=True)
                        return last
                    pe["w1", eh, c, b] = f
            for b in range(4):
                q0 = eh * QH + b * QB

                def f(e, i, w, eh=eh, b=b, q0=q0):
                    w("pe", ("w1", eh, C - 1, b))
                    w("dve", ("hr", eh, b - 1) if b else ("hr", 0, 3) if eh else ("eq", 1))
                    return e.tensor_tensor(hb[:].rearrange("p (q n) -> p q n", n=P), ps[:, b, :].rearrange("p (q n) -> p q n", n=P),
                                           b1c[:, q0:q0 + QB].unsqueeze(2).broadcast_to([P, QB, P]), ALU.add)
                dve["hb", eh, b] = f

                def f(e, i, w, eh=eh, b=b, q0=q0):
                    w("dve", ("hb", eh, b))
                    if eh == 0 and b == 0:
                        w("pe", ("w2", C - 1, NB - 1), 1)
                    for j in range(4):
                        last = e.tensor_scalar(hid[j * F:(j + 1) * F, q0:q0 + QB, j * NG:(j + 1) * NG],
                                               hb[j * F:(j + 1) * F, :].rearrange("p (q n) -> p q n", n=P)[:, :, j * NG:(j + 1) * NG],
                                               0.0, None, ALU.max)
                    return last
                dve["hr", eh, b] = f
        for n in loads:
            def f(e, i, w, n=n):
                kind = kinds[n // 4]
                if kind == "own":
                    own = [m for m in loads if kinds[m // 4] == "own" and m % 4 == n % 4]
                    m = own[own.index(n) - 1]
                    w("pe", ("w2", m // NB, m % NB), int(n < 4))
                    return e.dma_start(piece(n)[1], w2_dram[n // NB, n % NB])
                if kind[:3] == "res":
                    w("pe", ("sc", C - 1, 1), 1)
                else:
                    h = int(kind[-1])
                    w("pe", ("lg", h), -1)
                    w("pe", ("w1", 1, C - 2 + h, 3))
                return e.dma_start(rooms[kind].rearrange("p (b k) -> p b k", b=4),
                                   w2_dram[n // NB, n % NB:n % NB + 4].rearrange("b p k -> p b k"))
            sync["w2", n] = f
        for c in range(C):
            for b in range(NB):
                def f(e, i, w, c=c, b=b):
                    n = NB * c + b - 4
                    load, place = piece(NB * c + b)
                    w(slot(NB * c + b), load)
                    if n >= 0:
                        w("act", ("rs", n // NB, n % NB))
                    else:
                        w("dve" if b % 2 else "act", ("ga", 1, C - 1, b))
                    if c == 0 and (n >= 0 or b % 2 == 0):
                        w("dve", ("hr", b // 4, b % 4))
                    for j in range(QB):
                        q = QB * b + j
                        last = e.matmul(ps[:, 4 + b % 4, j * P:(j + 1) * P], hid[:, q, :],
                                        place[:, j * P:(j + 1) * P], start=True, stop=True)
                    return last
                pe["w2", c, b] = f

                def f(e, i, w, c=c, b=b):
                    w("pe", ("w2", c, b))
                    return e.activation(res[:, c % 2, b * 512:(b + 1) * 512], ps[:, 4 + b % 4, :], ACT.Copy)
                act["rs", c, b] = f

            def f(e, i, w, c=c):
                w("act", ("rs", c, NB - 1))
                v = res[:, c % 2, :].rearrange("p (q d) -> p d q", d=P)
                return e.transpose(v, v)
            dve["tr", c] = f
            for h in range(2):
                def f(e, i, w, c=c, h=h):
                    w("act", ("sel", 1), -1)
                    w("act", ("cp", h))
                    for t in range(TH):
                        tt = h * TH + t
                        last = e.matmul(ps[:, sbank(c, h), t * P:(t + 1) * P], selT[:, tt * P:(tt + 1) * P], b2s[:, c * P:(c + 1) * P],
                                        start=(t == 0), stop=False, skip_group_check=True)
                    return last
                if c == C - 1:
                    pe["bb", c, h] = f

                def f(e, i, w, c=c, h=h):
                    w("dve", ("tr", c))
                    r = res[:, c % 2, h * (Q // 2) * P:(h + 1) * (Q // 2) * P].rearrange("p (g d) -> p g d", d=P)
                    return e.tensor_tensor(r, r, b2s[:, c * P:(c + 1) * P].unsqueeze(1).broadcast_to([P, Q // 2, P]), ALU.add)
                if c < C - 1:
                    dve["b2", c, h] = f

                def f(e, i, w, c=c, h=h):
                    w("dve", ("b2", c, h) if c < C - 1 else ("tr", c))
                    if 0 < c < C - 1:
                        w("dve", ("fin", c - 1, h))
                    w("act", ("cp", h))
                    r = res[:, c % 2, :].rearrange("p (g d) -> p g d", d=P)
                    for t in range(TH):
                        tt = h * TH + t
                        for g in range(GT):
                            last = e.matmul(ps[g * G:(g + 1) * G, sbank(c, h), t * P:(t + 1) * P],
                                            selT[:, tt * P + g * G:tt * P + (g + 1) * G], r[:, tt * GT + g, :],
                                            start=(c < C - 1), stop=(c < C - 1 or (t == TH - 1 and g == GT - 1)),
                                            skip_group_check=True)
                    return last
                pe["sc", c, h] = f

                def f(e, i, w, c=c, h=h):
                    w("pe", ("sc", c, h))
                    w(f"y{h}", ("yl", c, h))
                    v = y[:, h].rearrange("p t d -> p (t d)")
                    return e.scalar_tensor_tensor(out=v, in0=ps[:, sbank(c, h), :], scalar=gate_f[:], in1=v, op0=ALU.mult, op1=ALU.add)
                dve["fin", c, h] = f

                def f(e, i, w, c=c, h=h):
                    w(f"s{h}", ("ys", (c - 1) % C, h), int(c == 0))
                    return e.dma_start(y[:, h], batch(x1_dram, i, h * TH, TH)[:, :, c * P:(c + 1) * P])
                sync["yl", c, h] = f

                def f(e, i, w, c=c, h=h):
                    w("dve", ("fin", c, h))
                    return e.dma_start(batch(out, i, h * TH, TH)[:, :, c * P:(c + 1) * P], y[:, h])
                sync["ys", c, h] = f

        ga = lambda eh, c, ks: [("ga", eh, c, k) for k in ks]
        allk, evenk, oddk = range(GB), range(0, GB, 2), range(1, GB, 2)

        pe_order, prev = [], None
        for eh in range(2):
            for c in range(C):
                if ("ga", eh, c) not in AHEAD:
                    pe_order += ga(eh, c, allk)
                if prev:
                    pe_order += [("w1",) + prev + (b,) for b in range(4)]
                prev = (eh, c)
        pe_order += [("w1",) + prev + (b,) for b in range(4)]
        after = {(0, 1): [("T", 0)], (0, 3): [("T", 1)], (0, 5): [("T", 2)], (0, 7): [("T", 3)],
                 (1, 1): [("lg", 0)], (1, 2): [("T", 4)], (1, 4): [("T", 5)], (1, 6): [("T", 6)], (2, 0): [("T", 7)],
                 (2, 2): [("lg", 1)], (2, 7): [("sT", 0)], (3, 0): [("sT", 1)]}
        for c in range(C):
            for b in range(NB):
                pe_order.append(("w2", c, b))
                pe_order += after.get((c, b), [])
            if c:
                pe_order += [("sc", c - 1, h) for h in range(2)]
        pe_order += ga(0, 0, allk) + ga(0, 1, allk) + [("bb", C - 1, h) for h in range(2)] + [("sc", C - 1, h) for h in range(2)]

        act_order = [("cp", 0), ("cp", 1)]
        for eh in range(2):
            for c in range(C):
                if ("ga", eh, c) not in AHEAD:
                    act_order += ga(eh, c, evenk)
        act_order += [(o, t) for t in range(2) for o in ("xf", "hi")] + [("hi", 2), ("hi", 3)]
        copies = []
        for c in range(C):
            for b in range(NB):
                copies.append(("rs", c, b))
                for o, *k in after.get((c, b), []):
                    if o == "T":
                        t = k[0]
                        copies.append(("xT", t))
                        if t + 2 < NT:
                            copies += [("xf", t + 2)] + ([("hi", t + 2)] if t + 2 >= 4 else [])
                    if o == "sT":
                        copies.append(("sel", k[0]))
        act_order += copies + ga(0, 0, allk) + ga(0, 1, allk)

        dve_order = []
        for eh in range(2):
            for c in range(C):
                if ("ga", eh, c) not in AHEAD:
                    dve_order += ga(eh, c, oddk)
                if (eh, c) == (0, 2):
                    dve_order += [("st", 0), ("st", 1), ("ag", 0), ("ag", 1), ("st", 2), ("st", 3), ("ag", 2), ("ag", 3)]
                if (eh, c) == (1, 0):
                    dve_order += [(o, 0, b) for b in range(4) for o in ("hb", "hr")]
        dve_order += [(o, 1, b) for b in range(4) for o in ("hb", "hr")]
        dve_order += [("st", 4), ("st", 5), ("ag", 4), ("ag", 5), ("st", 6), ("st", 7), ("ag", 6), ("ag", 7)]
        b2 = lambda c: [("b2", c, h) for h in range(2)]
        fin = lambda c: [("fin", c, h) for h in range(2)]
        dve_order += [("tr", 0)] + [("lg", 0), ("mx", 0), ("eq", 0)] + b2(0) + [("tr", 1)] + fin(0) + b2(1)
        dve_order += [("lg", 1), ("mx", 1), ("eq", 1), ("tr", 2)] + fin(1) + b2(2) + [("tr", 3)] + fin(2) + fin(3)

        pool_order = [("sp", 1, t) for t in range(NT)]
        norm = lambda k: [(o, k) for o in ("va", "r1", "ns", "nb")]
        pool_order += norm(0) + norm(1) + [("lo", 0), ("lo", 1)] + norm(2) + [("lo", 2), ("lo", 3)] + norm(3)
        pool_order += [("lo", t) for t in range(4, 8)] + [("sp", 0, t) for t in range(NT)]

        w2 = lambda *ns: [("w2", n) for n in ns]
        sync_order = [("x", t) for t in range(4)] + w2(0, 1, 2, 3) + [("yl", 0, 0), ("yl", 0, 1)] + w2(4, 8)
        ys = lambda c: [("ys", c, h) for h in range(2)]
        yl = lambda c: [("yl", c, h) for h in range(2)]
        sync_order += [("x", 4), ("x", 5), ("x", 6)] + w2(12, 13, 14, 15) + [("x", 7)] + w2(16, 20, 21, 22, 23)
        sync_order += ys(0) + yl(1) + w2(24, 28, 29, 30, 31) + ys(1) + yl(2) + ys(2) + yl(3) + ys(3)

        slots = {f"x{k}": [("x", k), ("x", k + 4)] for k in range(4)}
        for n in loads:
            slots.setdefault(slot(n), []).append(("w2", n))
        slots |= {f"y{h}": [("yl", c, h) for c in range(C)] for h in range(2)}
        slots |= {f"s{h}": [("ys", c, h) for c in range(C)] for h in range(2)}
        plans = {"pe": (pe, pe_order), "act": (act, act_order), "dve": (dve, dve_order), "pool": (pool, pool_order),
                 "sync": (sync, sync_order)}
        Phase(nc, sem, "b", {k: [(n, d[n]) for n in o] for k, (d, o) in plans.items()}, slots, lead, B)


def kernel(x, ctx_1024, mask_BxS2_bk0, g_xattn, g_ffn, L0_xattn_rms_scale, L0_xattn_q_w, L0_xattn_kv_w,
           L0_xattn_out_w, L0_ffn_Wc, L0_ffn_bc, L0_ffn_W1, L0_ffn_b1, L0_ffn_W2, L0_ffn_b2):
    from concourse import bacc
    from concourse.bass_utils import run_bass_kernel_spmd

    half = np.arange(DH // 2, dtype=np.float32)
    scale = np.float32(10000.0) ** (np.float32(2.0 / DH) * half)
    angle = np.arange(S + T, dtype=np.float32)[None, :] / scale[:, None]
    cos = np.concatenate([np.cos(angle), np.cos(angle)]).astype(np.float32)
    sin = np.concatenate([np.sin(angle), -np.sin(angle)]).astype(np.float32)
    tie = np.linspace(0.0, 1e-6, G, dtype=np.float32)
    gmask = np.repeat(np.eye(GT, dtype=np.float32), G, axis=0)

    w1 = np.asarray(L0_ffn_W1).reshape(4, Q, C, P, F).transpose(3, 2, 1, 0, 4).reshape(P, C, E * F)
    w2 = np.asarray(L0_ffn_W2).reshape(4, Q // QB, QB, C, P, F).transpose(3, 1, 0, 5, 2, 4).reshape(C, Q // QB, P, QB * P)
    b1 = np.asarray(L0_ffn_b1).reshape(4, Q, F).transpose(0, 2, 1).reshape(P, Q)

    arrays = {
        "x": x, "ctx_1024": ctx_1024, "mask": np.asarray(mask_BxS2_bk0).T, "g_xattn": g_xattn, "g_ffn": g_ffn,
        "rms": np.asarray(L0_xattn_rms_scale).reshape(C, P).T, "q_w": L0_xattn_q_w, "kv_w": L0_xattn_kv_w, "out_w": L0_xattn_out_w,
        "Wc": L0_ffn_Wc, "bc": np.asarray(L0_ffn_bc).reshape(E, 1), "W1": w1, "b1": b1, "W2": w2, "b2": L0_ffn_b2,
        "ident": np.eye(P, dtype=np.float32), "cos": cos, "sin": sin, "tie": tie, "gmask": gmask,
    }
    arrays = {n: np.ascontiguousarray(a) for n, a in arrays.items()}
    nc = bacc.Bacc("TRN2", target_bir_lowering=False, num_devices=1)
    args = [nc.dram_tensor(f"in_{n}", a.shape, mybir.dt.from_np(a.dtype), kind="ExternalInput").ap() for n, a in arrays.items()]
    out = nc.dram_tensor("out", (B, T, D), F32, kind="ExternalOutput").ap()
    build(nc, *args, out)
    r = run_bass_kernel_spmd(nc, [{f"in_{n}": a for n, a in arrays.items()}], core_ids=[0])
    return r.results[0]["out"]
```
